# Optimizing a Trainium2 kernel written in Bass

```python
import numpy as np
import jax
import jax.numpy as jnp

def _softmax(x, axis=-1):
    return jax.nn.softmax(x, axis=axis)

def _gelu(x):
    return jax.nn.gelu(x, approximate=True)

def _silu(x):
    return jax.nn.silu(x)

def _sigmoid(x):
    return jax.nn.sigmoid(x)

def _layernorm(x, axis=-1, eps=1e-05):
    m = jnp.mean(x, axis=axis, keepdims=True)
    v = jnp.var(x, axis=axis, keepdims=True)
    return (x - m) / jnp.sqrt(v + eps)

def _scatter_add(tgt, idx, src, axis=0):
    return tgt.at[idx].add(src)

def _segment_sum(src, seg, n):
    return jax.ops.segment_sum(src, seg, n)
kernel_name = 'mk_hybrid_d1_jaxref_r8_ad6368'

def setup_inputs(seed: int=0):
    np.random.seed(seed)
    _w = jnp.asarray

    def _L0_attn_a_setup():
        import jax, jax.numpy as jnp
        import numpy as np
        B, L, D, H = (2, 256, 128, 16)
        HD = D // H
        ROPE_BASE = 10000.0

        def _rope(x):
            seq, hd = (x.shape[2], x.shape[3])
            inv_freq = 1.0 / ROPE_BASE ** (jnp.arange(0, hd, 2, dtype=jnp.float32) / hd)
            freqs = jnp.arange(seq, dtype=jnp.float32)[:, None] * inv_freq
            cos = jnp.repeat(jnp.cos(freqs), 2, axis=-1)
            sin = jnp.repeat(jnp.sin(freqs), 2, axis=-1)
            xp = x.reshape(*x.shape[:-1], hd // 2, 2)
            x_rot = jnp.stack([-xp[..., 1], xp[..., 0]], axis=-1).reshape(x.shape)
            return x * cos + x_rot * sin
        key = jax.random.key(seed)
        ks = jax.random.split(key, 9)
        s = 1.0 / np.sqrt(D)
        mk = lambda k: jax.random.normal(k, (D, D), dtype=jnp.float32) * s
        return {'x': jax.random.normal(ks[0], (B, L, D), dtype=jnp.float32), 'Wq': mk(ks[1]), 'bq': jnp.zeros((D,), jnp.float32), 'Wk': mk(ks[2]), 'bk': jnp.zeros((D,), jnp.float32), 'Wv': mk(ks[3]), 'bv': jnp.zeros((D,), jnp.float32), 'Wp': mk(ks[4]), 'bp': jnp.zeros((D,), jnp.float32)}
    _L0_attn_a_in = _L0_attn_a_setup()

    def _L0_attn_b_setup():
        import jax, jax.numpy as jnp
        import numpy as np
        D_MODEL = 128
        NUM_HEADS = 16
        D_K = D_MODEL // NUM_HEADS
        key = jax.random.key(seed)
        k1, k2, k3, k4, k5 = jax.random.split(key, 5)
        scale = 1.0 / np.sqrt(D_MODEL)
        x = jax.random.normal(k1, (2, 1024, D_MODEL), dtype=jnp.float32)
        W_qkv = jax.random.normal(k2, (D_MODEL, 3 * D_MODEL), dtype=jnp.float32) * scale
        b_qkv = jax.random.normal(k3, (3 * D_MODEL,), dtype=jnp.float32) * 0.01
        W_out = jax.random.normal(k4, (D_MODEL, D_MODEL), dtype=jnp.float32) * scale
        b_out = jax.random.normal(k5, (D_MODEL,), dtype=jnp.float32) * 0.01
        return {'x': x, 'W_qkv': W_qkv, 'b_qkv': b_qkv, 'W_out': W_out, 'b_out': b_out}
    _L0_attn_b_in = _L0_attn_b_setup()

    def _L0_ffn_setup():
        import jax, jax.numpy as jnp
        import numpy as np
        DIM = 128

        def _reference_tuple_inner(x, W_r, W_k, W_v, mu_r, mu_k):
            B, T, C = x.shape
            x_prev = jnp.concatenate([jnp.zeros((B, 1, C), x.dtype), x[:, :-1, :]], axis=1)
            xr = mu_r * x + (1.0 - mu_r) * x_prev
            xk = mu_k * x + (1.0 - mu_k) * x_prev
            r = jax.nn.sigmoid(jnp.einsum('btc,dc->btd', xr, W_r))
            k = jnp.einsum('btc,dc->btd', xk, W_k)
            k_act = jnp.square(jax.nn.relu(k))
            out = r * jnp.einsum('btc,dc->btd', k_act, W_v)
            new_state = x[:, -1, :]
            return (out, new_state)
        key = jax.random.key(seed)
        ks = jax.random.split(key, 6)
        B, T, C = (8, 256, DIM)
        x = jax.random.normal(ks[0], (B, T, C), dtype=jnp.float32)
        s = 1.0 / np.sqrt(C)
        W_r = jax.random.uniform(ks[1], (C, C), jnp.float32, -s, s)
        W_k = jax.random.uniform(ks[2], (C, C), jnp.float32, -s, s)
        W_v = jax.random.uniform(ks[3], (C, C), jnp.float32, -s, s)
        mu_r = jax.random.uniform(ks[4], (C,), jnp.float32)
        mu_k = jax.random.uniform(ks[5], (C,), jnp.float32)
        return {'x': x, 'W_r': W_r, 'W_k': W_k, 'W_v': W_v, 'mu_r': mu_r, 'mu_k': mu_k}
    _L0_ffn_in = _L0_ffn_setup()
    _d = {'L0_attn_a_x': _L0_attn_a_in['x'], 'L0_attn_a_Wq': _L0_attn_a_in['Wq'], 'L0_attn_a_bq': _L0_attn_a_in['bq'], 'L0_attn_a_Wk': _L0_attn_a_in['Wk'], 'L0_attn_a_bk': _L0_attn_a_in['bk'], 'L0_attn_a_Wv': _L0_attn_a_in['Wv'], 'L0_attn_a_bv': _L0_attn_a_in['bv'], 'L0_attn_a_Wp': _L0_attn_a_in['Wp'], 'L0_attn_a_bp': _L0_attn_a_in['bp'], 'L0_attn_b_W_qkv': _L0_attn_b_in['W_qkv'], 'L0_attn_b_b_qkv': _L0_attn_b_in['b_qkv'], 'L0_attn_b_W_out': _L0_attn_b_in['W_out'], 'L0_attn_b_b_out': _L0_attn_b_in['b_out'], 'L0_ffn_W_r': _L0_ffn_in['W_r'], 'L0_ffn_W_k': _L0_ffn_in['W_k'], 'L0_ffn_W_v': _L0_ffn_in['W_v'], 'L0_ffn_mu_r': _L0_ffn_in['mu_r'], 'L0_ffn_mu_k': _L0_ffn_in['mu_k']}
    _x0 = _d['L0_attn_a_x']
    _d['L0_attn_a_x'] = jax.random.normal(jax.random.fold_in(jax.random.key(seed), 1), (1, 2048, 128), dtype=_x0.dtype)
    del _x0
    return _d

def reference(L0_attn_a_x, L0_attn_a_Wq, L0_attn_a_bq, L0_attn_a_Wk, L0_attn_a_bk, L0_attn_a_Wv, L0_attn_a_bv, L0_attn_a_Wp, L0_attn_a_bp, L0_attn_b_W_qkv, L0_attn_b_b_qkv, L0_attn_b_W_out, L0_attn_b_b_out, L0_ffn_W_r, L0_ffn_W_k, L0_ffn_W_v, L0_ffn_mu_r, L0_ffn_mu_k):

    def _L0_attn_a_ref(x, Wq, bq, Wk, bk, Wv, bv, Wp, bp):
        import jax, jax.numpy as jnp
        import numpy as np
        B, L, D, H = (2, 256, 128, 16)
        HD = D // H
        ROPE_BASE = 10000.0

        def _rope(x):
            seq, hd = (x.shape[2], x.shape[3])
            inv_freq = 1.0 / ROPE_BASE ** (jnp.arange(0, hd, 2, dtype=jnp.float32) / hd)
            freqs = jnp.arange(seq, dtype=jnp.float32)[:, None] * inv_freq
            cos = jnp.repeat(jnp.cos(freqs), 2, axis=-1)
            sin = jnp.repeat(jnp.sin(freqs), 2, axis=-1)
            xp = x.reshape(*x.shape[:-1], hd // 2, 2)
            x_rot = jnp.stack([-xp[..., 1], xp[..., 0]], axis=-1).reshape(x.shape)
            return x * cos + x_rot * sin
        b, l, d = x.shape
        to_heads = lambda t: t.reshape(b, l, H, HD).transpose(0, 2, 1, 3)
        q = to_heads(x @ Wq + bq)
        k = to_heads(x @ Wk + bk)
        v = to_heads(x @ Wv + bv)
        q = _rope(q)
        k = _rope(k)
        scores = jnp.einsum('bhic,bhjc->bhij', q, k) / np.sqrt(HD)
        attn = jax.nn.softmax(scores, axis=-1)
        out = jnp.einsum('bhij,bhjc->bhic', attn, v)
        out = out.transpose(0, 2, 1, 3).reshape(b, l, d)
        return out @ Wp + bp

    def _L0_attn_b_ref(x, W_qkv, b_qkv, W_out, b_out):
        import jax, jax.numpy as jnp
        import numpy as np
        D_MODEL = 128
        NUM_HEADS = 16
        D_K = D_MODEL // NUM_HEADS
        B, S, _ = x.shape
        qkv = (jnp.einsum('bsd,de->bse', x, W_qkv) + b_qkv).reshape(B, S, NUM_HEADS, 3 * D_K)
        q, k, v = (qkv[..., :D_K], qkv[..., D_K:2 * D_K], qkv[..., 2 * D_K:])
        scores = jnp.einsum('bshd,bsgd->bshg', q, k) / np.sqrt(D_K)
        attn = jax.nn.softmax(scores, axis=-1)
        context = jnp.einsum('bshg,bsgd->bshd', attn, v).reshape(B, S, NUM_HEADS * D_K)
        return jnp.einsum('bsd,de->bse', context, W_out) + b_out

    def _L0_ffn_ref(x, W_r, W_k, W_v, mu_r, mu_k):
        import jax, jax.numpy as jnp
        import numpy as np
        DIM = 128

        def _reference_tuple_inner(x, W_r, W_k, W_v, mu_r, mu_k):
            B, T, C = x.shape
            x_prev = jnp.concatenate([jnp.zeros((B, 1, C), x.dtype), x[:, :-1, :]], axis=1)
            xr = mu_r * x + (1.0 - mu_r) * x_prev
            xk = mu_k * x + (1.0 - mu_k) * x_prev
            r = jax.nn.sigmoid(jnp.einsum('btc,dc->btd', xr, W_r))
            k = jnp.einsum('btc,dc->btd', xk, W_k)
            k_act = jnp.square(jax.nn.relu(k))
            out = r * jnp.einsum('btc,dc->btd', k_act, W_v)
            new_state = x[:, -1, :]
            return (out, new_state)
        return _reference_tuple_inner(x, W_r, W_k, W_v, mu_r, mu_k)[0]
    x = L0_attn_a_x
    x = x + _L0_attn_a_ref(_layernorm(x, axis=-1), L0_attn_a_Wq, L0_attn_a_bq, L0_attn_a_Wk, L0_attn_a_bk, L0_attn_a_Wv, L0_attn_a_bv, L0_attn_a_Wp, L0_attn_a_bp)
    x = x + _L0_ffn_ref(_layernorm(x, axis=-1), L0_ffn_W_r, L0_ffn_W_k, L0_ffn_W_v, L0_ffn_mu_r, L0_ffn_mu_k)
    x = x + _L0_attn_b_ref(_layernorm(x, axis=-1), L0_attn_b_W_qkv, L0_attn_b_b_qkv, L0_attn_b_W_out, L0_attn_b_b_out)
    x = x + _L0_ffn_ref(_layernorm(x, axis=-1), L0_ffn_W_r, L0_ffn_W_k, L0_ffn_W_v, L0_ffn_mu_r, L0_ffn_mu_k)
    return x

_drawn_inputs = setup_inputs


def setup_inputs(seed=0):
    import zlib

    import numpy as np

    out = dict(_drawn_inputs(seed))
    spreads = {'L0_attn_a_bq': (0.0, 0.8),
     'L0_attn_a_bk': (0.0, 0.8),
     'L0_attn_a_bv': (0.0, 0.1),
     'L0_attn_a_bp': (0.0, 0.1)}
    factors = {'L0_attn_b_b_qkv': 8.0, 'L0_attn_b_b_out': 5.996, 'L0_ffn_mu_r': 3.368}
    for name, (base, spread) in spreads.items():
        noise = np.random.default_rng([zlib.crc32(name.encode()), seed]).standard_normal(out[name].shape)
        drawn = base * np.exp(spread * noise) if base else spread * noise
        out[name] = jnp.asarray(drawn.astype(out[name].dtype))
    for name, factor in factors.items():
        out[name] = (out[name] * factor).astype(out[name].dtype)
    return out
```

```python
from contextlib import ExitStack

import numpy as np

import concourse.bass as bass
from concourse import mybir

F32 = mybir.dt.float32
BF16 = mybir.dt.bfloat16
ALU = mybir.AluOpType
ACT = mybir.ActivationFunctionType
AX_X = mybir.AxisListType.X

P = 128
S = 2048
H, HD = 16, 8
TILES = S // P
CHUNK = 512
CHUNKS = S // CHUNK
TPC = CHUNK // P
HG = 4
GROUPS = H // HG
UNITS = GROUPS * CHUNKS
STEPS = TILES
ROWS = HG * TPC
KC = S // CHUNK
LEAD = 4
LAG = 2
RING = 4
VW = HD + 1
STRIP = 32
PARTS_Q = (0, 0, 1, 0, 2, 1)
PARTS_K = (0, 1, 0, 2, 0, 1)
MROW = 64
SCALE = float(1.0 / np.sqrt(HD))
EPS = 1e-5
ROPE_BASE = 10000.0

(BQ, BK, BQ_SWAP, BK_SWAP, MU_R, MU_K, BV, BP, B_OUT, B_QKV) = range(10)
N_COLS = 6
N_ROWS = 12


def build(nc, x_in, wq, bq, wk, bk, wv, bv, wp, bp, w_qkv, b_qkv, w_out, b_out,
          w_r, w_k, w_v, mu_r, mu_k, cos_t, sin_t, zero_rows, out):
    with ExitStack() as ctx:
        def sb(name, shape, dt):
            return ctx.enter_context(nc.sbuf_tensor(name, shape, dt))

        def sem(name):
            return ctx.enter_context(nc.semaphore(name))

        psum = ctx.enter_context(nc.psum_tensor("psum", [P, 8, CHUNK], F32))

        x = sb("x", [P, TILES, P], F32)
        xnT = sb("xnT", [P, 1 + S], F32)
        attn = sb("attn", [P, TILES, P], F32)
        xn = attn
        kst = sb("kst", [P, 2 * HG * S], BF16)
        qst = sb("qst", [P, 2, HG, CHUNKS, CHUNK], BF16)
        qflat = qst[:].rearrange("p a j c t -> p (a j c t)")
        probs = sb("probs", [P, RING, HG * CHUNK], F32)
        v_all = sb("v_all", [P, GROUPS * TILES * HG * VW], F32)
        v_unit = sb("v_unit", [P, TILES, HG, STRIP], F32)
        o_unit = sb("o_unit", [P, CHUNK], F32)
        parts = [sb("k_parts", [P, 3, S], BF16), sb("q_parts", [P, 3, S], BF16)]

        def in_probs(slot, half):
            return probs[:, slot, half * 2 * CHUNK:(half + 1) * 2 * CHUNK].rearrange("p (b t) -> p b t", b=2)

        cos = probs[:, 0, :]
        sin = probs[:, 1, :]
        comb = in_probs(2, 0)
        rope1 = in_probs(2, 1)[:, 0, :]
        rope2 = in_probs(2, 1)[:, 1, :]
        resid = in_probs(3, 0)
        ffn_r = in_probs(0, 0)
        ffn_k = in_probs(0, 1)
        gate = in_probs(1, 0)
        relu = in_probs(1, 1)
        act2 = in_probs(2, 0)
        qkv = kst[:].bitcast(F32)[:, 0:TILES * 3 * P].rearrange("p (n e) -> p n e", n=TILES)
        prod = probs[:, 0:3, :]
        hs = qflat.bitcast(F32)[:, 0:TILES * H * H].rearrange("p (n e) -> p n e", n=TILES)
        he = qflat.bitcast(F32)[:, TILES * H * H:2 * TILES * H * H].rearrange("p (n e) -> p n e", n=TILES)
        ctx_raw = probs[:, 3, :].rearrange("p (n e) -> p n e", n=TILES)
        hmax = sb("hmax", [P, TPC * H], F32)
        hden = sb("hden", [P, TPC * H], F32)
        hrden = sb("hrden", [P, TPC * H], F32)
        wa = sb("wa", [P, 4, P], F32)
        wsw = sb("wsw", [P, 2, P], F32)
        wqkv = sb("wqkv", [P, 3 * P], F32)
        wout = sb("wout", [P, P], F32)
        wf_in = sb("wf_in", [P, 3, P], F32)
        wfT = sb("wfT", [P, 3, P], F32)
        rows = sb("rows", [1, N_ROWS, P], F32)
        cols = sb("cols", [P, N_COLS], F32)
        omu = sb("omu", [P, 2], F32)
        bcast = sb("bcast", [P, 3, P], F32)
        ident = sb("ident", [P, P], F32)
        ident_b = sb("ident_b", [P, P], BF16)
        ones_row = sb("ones_row", [1, P], F32)
        stats = sb("stats", [P, TILES, 6], F32)
        mv = sb("mv", [P, TILES, 2], F32)
        veps = sb("veps", [P, TILES], F32)
        std = sb("std", [P, TILES], F32)
        rstd = sb("rstd", [P, TILES], F32)
        mpart = sb("mpart", [P, ROWS * KC], F32)
        nmax = sb("nmax", [P, ROWS], F32)
        nmax_r = sb("nmax_r", [P, 2, ROWS], F32)
        nmax_p = sb("nmax_p", [P, ROWS, 3], BF16)
        rden = sb("rden", [P, TPC * HG], F32)

        scratch = [nc.dram_tensor("k_scratch", (3, P, S), BF16, kind="Internal").ap(),
                   nc.dram_tensor("q_scratch", (3, P, S), BF16, kind="Internal").ap()]

        x_loaded = sem("x_loaded")
        w_loaded = sem("w_loaded")
        rows_loaded = sem("rows_loaded")
        trig_loaded = sem("trig_loaded")
        pool_step = sem("pool_step")
        ident_ready = sem("ident_ready")
        zeroed = sem("zeroed")
        rows_done = sem("rows_done")
        weights_turned = sem("weights_turned")
        vectors_spread = sem("vectors_spread")
        weights_done = sem("weights_done")
        vectors_done = sem("vectors_done")
        dve_step = sem("dve_step")
        var_ready = sem("var_ready")
        std_ready = sem("std_ready")
        xn_ready = sem("xn_ready")
        turned = sem("turned")
        turned_copied = sem("turned_copied")
        proj_ready = sem("proj_ready")
        comb_ready = sem("comb_ready")
        hi_ready = sem("hi_ready")
        resid_ready = sem("resid_ready")
        mid_ready = sem("mid_ready")
        lo_ready = sem("lo_ready")
        v_ready = sem("v_ready")
        v_used = sem("v_used")
        scratch_written = sem("scratch_written")
        stack_loading = sem("stack_loading")
        stacks_ready = sem("stacks_ready")
        sm_ready = sem("sm_ready")
        sm_free = sem("sm_free")
        st_ready = sem("st_ready")
        exp_done = sem("exp_done")
        pv_done = sem("pv_done")
        v_unit_ready = sem("v_unit_ready")
        o_copied = sem("o_copied")
        o_turned = sem("o_turned")
        rden_ready = sem("rden_ready")
        o_done = sem("o_done")
        max_step = sem("max_step")
        max_turned = sem("max_turned")
        max_copied = sem("max_copied")
        qkv_ready = sem("qkv_ready")
        qkv_copied = sem("qkv_copied")
        hs_ready = sem("hs_ready")
        he_ready = sem("he_ready")
        ctx_ready = sem("ctx_ready")
        xb_ready = sem("xb_ready")
        op_ready = sem("op_ready")
        x_new = sem("x_new")
        mixed = sem("mixed")
        rk_ready = sem("rk_ready")
        gate_ready = sem("gate_ready")
        relu_ready = sem("relu_ready")
        act_ready = sem("act_ready")
        kv_ready = sem("kv_ready")
        stored = sem("stored")

        MSTEPS = 6

        def turn_bank(c):
            return psum[:, c % 2, :]

        def proj_bank(n):
            return psum[:, 2 + n % 2, :]

        def swap_bank(n):
            return psum[:, 4 + n % 2, :]

        def out_bank(c):
            return psum[:, 6 + c % 2, :]

        def qkv_bank(n):
            return psum[:, 2 + n % 4, 0:3 * P]

        def st_bank(pair, jj):
            return psum[:, 2 * pair + jj, :]

        def st_pair(pair):
            return psum[:, 2 * pair:2 * pair + 2, :]

        def sm_bank(kc):
            return psum[:, 4 + kc % 2, :]

        acc = psum[:, 6, :]
        misc = psum[:, 7, :]
        misc_b = misc.bitcast(BF16)
        misc_o = misc.rearrange("p (q j e) -> p q j e", q=TPC, j=HG)

        def k_cols(unit, j, first, n):
            return kst[:, bass.ds(((unit // CHUNKS) % 2) * (HG * S) + (j * S + first), n)]

        def q_cols(unit, j, first, n):
            return qflat[:, bass.ds(((unit // CHUNKS) % 2) * (HG * S) + (unit % CHUNKS) * CHUNK + (j * S + first), n)]

        def max_row(unit, t):
            return (unit + 1, t + LEAD) if t < STEPS - LEAD else (unit + 2, t + LEAD - STEPS)

        def attention_units(eng, body):
            body(0, True, True, False)
            with eng.Fori(1, UNITS - 2) as unit:
                body(unit, True, True, True)
            body(UNITS - 2, True, False, True)
            body(UNITS - 1, False, False, True)

        block = ctx.enter_context(nc.Block())

        @block.sync
        def _(sp):
            for c in range(CHUNKS):
                src = x_in[c * CHUNK:(c + 1) * CHUNK, :].rearrange("(n p) d -> p n d", p=P)
                sp.dma_start(x[:, c * TPC:(c + 1) * TPC, :], src).then_inc(x_loaded, 16)
            for i, w in enumerate((wq, wk, wv, wp)):
                sp.dma_start(wa[:, i, :], w).then_inc(w_loaded, 16)
            sp.dma_start(wqkv[:], w_qkv).then_inc(w_loaded, 16)
            sp.dma_start(wout[:], w_out).then_inc(w_loaded, 16)
            for i, w in enumerate((w_r, w_k, w_v)):
                sp.dma_start(wf_in[:, i, :], w).then_inc(w_loaded, 16)
            sp.dma_start(cos, cos_t).then_inc(trig_loaded, 16)
            sp.dma_start(sin, sin_t).then_inc(trig_loaded, 16)

            for n in range(2 * CHUNKS):
                c, kq = n // 2, n % 2
                sp.wait_ge(lo_ready, n + 1)
                cs = slice(c * CHUNK, (c + 1) * CHUNK)
                sp.dma_start(scratch[kq][:, :, cs].rearrange("s p t -> p s t"),
                             parts[kq][:, :, cs]).then_inc(scratch_written, 16)
            sp.wait_ge(scratch_written, 2 * CHUNKS * 16)
            sp.wait_ge(zeroed, 1)
            for g in range(GROUPS):
                half = g % 2
                if g >= 2:
                    sp.wait_ge(exp_done, 2 + 2 * STEPS * CHUNKS * (g - 1))
                heads = slice(g * HG * HD, (g + 1) * HG * HD)
                kdst = kst[:].rearrange("p (a j t) -> p a j t", a=2, j=HG)
                for slot in range(len(PARTS_K)):
                    at = slice(HD * slot, HD * slot + HD)
                    sp.dma_start(kdst[at, half], scratch[0][PARTS_K[slot], heads, :].rearrange(
                        "(j d) t -> d j t", j=HG)).then_inc(stack_loading, 16)
                    sp.dma_start(qst[at, half].rearrange("p j c t -> p j (c t)"),
                                 scratch[1][PARTS_Q[slot], heads, :].rearrange(
                                     "(j d) t -> d j t", j=HG)).then_inc(stack_loading, 16)
                sp.dma_start(qst[MROW:MROW + 3, half].rearrange("p j c t -> p (j c t)").bitcast(F32),
                             zero_rows).then_inc(stack_loading, 16)
                sp.wait_ge(stack_loading, 13 * 16 * (g + 1))
                sp.sem_inc(stacks_ready, 1)
            for c in range(CHUNKS):
                sp.wait_ge(x_new, 3 * CHUNKS + c + 1)
                dst = out[c * CHUNK:(c + 1) * CHUNK, :].rearrange("(n p) d -> p n d", p=P)
                sp.dma_start(dst, x[:, c * TPC:(c + 1) * TPC, :]).then_inc(stored, 16)
            sp.wait_ge(stored, 16 * CHUNKS)

        @block.gpsimd
        def _(pool):
            def row(slot, src):
                pool.dma_start(rows[0:1, slot, :], src).then_inc(rows_loaded, 16)

            for slot, v in ((BQ, bq), (BK, bk), (BV, bv), (BP, bp), (B_OUT, b_out), (MU_R, mu_r), (MU_K, mu_k)):
                row(slot, v.rearrange("(a d) -> a d", a=1))
            pool.dma_start(rows[0:1, B_QKV:N_ROWS, :].rearrange("p k d -> p (k d)"),
                           b_qkv.rearrange("(a d) -> a d", a=1)).then_inc(rows_loaded, 16)
            pool.memset(ident[:], 0.0).then_inc(pool_step, 1)
            pool.memset(ones_row[:], 1.0).then_inc(pool_step, 1)
            pool.wait_ge(pool_step, 2)
            pool.affine_select(out=ident[:], in_=ident[:], compare_op=ALU.not_equal, fill=1.0, base=0,
                               pattern=[[-1, P]], channel_multiplier=1).then_inc(pool_step, 1)
            pool.wait_ge(pool_step, 3)
            pool.tensor_copy(ident_b[:], ident[:]).then_inc(ident_ready, 1)
            pool.memset(kst[:].bitcast(F32), 0.0).then_inc(pool_step, 1)
            pool.memset(qflat.bitcast(F32), 0.0).then_inc(pool_step, 1)
            pool.memset(v_unit[:], 0.0).then_inc(pool_step, 1)
            pool.wait_ge(pool_step, 6)
            pool.memset(kst[MROW:MROW + 3, :], 1.0).then_inc(zeroed, 1)
            pool.wait_ge(zeroed, 1)
            pool.wait_ge(vectors_done, 1)
            pool.wait_ge(xn_ready, CHUNKS)
            pool.tensor_tensor(x[:], x[:], bcast[:, 1, :].unsqueeze(1).to_broadcast([P, TILES, P]),
                               ALU.add).then_inc(xb_ready, 1)
            pool.wait_ge(v_used, CHUNKS)
            with pool.Fori(0, UNITS) as unit:
                pool.wait_ge(pv_done, unit * STEPS + RING)
                pool.tensor_copy(
                    v_unit[:, :, :, 0:VW],
                    v_all[:, bass.ds((unit // CHUNKS) * (TILES * HG * VW), TILES * HG * VW)].rearrange(
                        "p (t j e) -> p t j e", t=TILES, j=HG)).then_inc(v_unit_ready, 1)
            pool.wait_ge(xn_ready, 3 * CHUNKS)
            pool.tensor_tensor(x[:], x[:], bcast[:, 2, :].unsqueeze(1).to_broadcast([P, TILES, P]),
                               ALU.add).then_inc(xb_ready, 1)

        @block.scalar
        def _(act):
            act.sem_inc(exp_done, 2)

            def weights():
                act.wait_ge(w_loaded, 9 * 16)
                for i in range(2):
                    pair = wa[:, i, :].rearrange("p (n two) -> p n two", two=2)
                    swap = wsw[:, i, :].rearrange("p (n two) -> p n two", two=2)
                    act.copy(swap[:, :, 0], pair[:, :, 1])
                    act.copy(swap[:, :, 1], pair[:, :, 0])
                act.wait_ge(weights_turned, 1)
                act.copy(wfT[:].rearrange("p k n -> p (k n)"), out_bank(1)[:, 0:3 * P]).then_inc(weights_done, 1)

            def layer_norm(layer):
                act.wait_ge(var_ready, layer + 1)
                act.activation(std[:], veps[:], ACT.Sqrt).then_inc(std_ready, 1)
                for c in range(CHUNKS):
                    copy_turned(CHUNKS * (layer + (layer + 1) // 2) + c, c)

            def copy_turned(n, c):
                act.wait_ge(turned, n + 1)
                act.copy(xnT[:, 1 + c * CHUNK:1 + (c + 1) * CHUNK], turn_bank(c)).then_inc(turned_copied, 1)

            def split():
                for n in range(2 * CHUNKS + 1):
                    if n < 2 * CHUNKS:
                        c, kq = n // 2, n % 2
                        act.wait_ge(comb_ready, n + 1)
                        act.copy(parts[kq][:, 0, c * CHUNK:(c + 1) * CHUNK], comb[:, n % 2, :]).then_inc(hi_ready, 1)
                    if n >= 1:
                        c, kq = (n - 1) // 2, (n - 1) % 2
                        act.wait_ge(resid_ready, n)
                        act.copy(parts[kq][:, 1, c * CHUNK:(c + 1) * CHUNK],
                                 resid[:, (n - 1) % 2, :]).then_inc(mid_ready, 1)

            def copy_max(unit, half):
                act.wait_ge(max_turned, unit * 2 + (half + 1))
                act.copy(qst[MROW:MROW + 3, bass.ds((unit // CHUNKS) % 2, 1), 2 * half:2 * half + 2,
                             bass.ds(unit % CHUNKS, 1), :],
                         misc_b[MROW:MROW + 3, :].rearrange("p (a j c t) -> p a j c t", a=1, j=2, c=1)
                         ).then_inc(max_copied, 1)

            def unit_body(unit, has_next, has_second, has_before):
                for t in range(STEPS):
                    for pair in range(2):
                        act.wait_ge(st_ready, unit * 2 * STEPS + (2 * t + pair + 1))
                        if pair == 0:
                            act.wait_ge(pv_done, unit * STEPS + (t + 1))
                        act.activation(probs[:, t % RING, pair * 2 * CHUNK:(pair + 1) * 2 * CHUNK],
                                       st_pair(pair).rearrange("p a t -> p (a t)"),
                                       ACT.Exp, scale=SCALE).then_inc(exp_done, 1)
                    if t == 0 and has_before:
                        act.wait_ge(pv_done, unit * STEPS + RING)
                        act.copy(o_unit[:], acc).then_inc(o_copied, 1)
                    if has_next and t in (STEPS - 3, STEPS - 2):
                        copy_max(unit + 1, t - (STEPS - 3))

            def finish_attention(c0):
                for c in range(CHUNKS):
                    copy_turned(c0 + c, c)

            def ffn(f):
                for c in range(CHUNKS):
                    n = CHUNKS * f + c
                    act.wait_ge(rk_ready, n + 1)
                    if c >= 2:
                        act.wait_ge(x_new, CHUNKS * (2 * f + 1) + c - 1)
                        act.wait_ge(kv_ready, n - 1)
                    act.activation(gate[:, c % 2, :], proj_bank(c), ACT.Sigmoid).then_inc(gate_ready, 1)
                    act.activation(relu[:, c % 2, :], swap_bank(c), ACT.Relu).then_inc(relu_ready, 1)
                    act.wait_ge(relu_ready, n + 1)
                    act.activation(act2[:, c % 2, :], relu[:, c % 2, :], ACT.Square).then_inc(act_ready, 1)

            def head_attention():
                for c in range(CHUNKS + 1):
                    for i in range(TPC if c < CHUNKS else 0):
                        n = TPC * c + i
                        act.wait_ge(qkv_ready, n + 1)
                        act.copy(qkv[:, n, :], qkv_bank(n)).then_inc(qkv_copied, 1)
                for c in range(CHUNKS):
                    act.wait_ge(hs_ready, c + 1)
                    act.activation(he[:, c * TPC:(c + 1) * TPC, :], hs[:, c * TPC:(c + 1) * TPC, :],
                                   ACT.Exp, scale=SCALE).then_inc(he_ready, 1)

            layer_norm(0)
            weights()
            split()
            copy_max(0, 0)
            copy_max(0, 1)
            attention_units(act, unit_body)
            act.wait_ge(pv_done, UNITS * STEPS + RING)
            act.copy(o_unit[:], acc).then_inc(o_copied, 1)
            finish_attention(CHUNKS)
            layer_norm(1)
            ffn(0)
            layer_norm(2)
            head_attention()
            finish_attention(4 * CHUNKS)
            layer_norm(3)
            ffn(1)

        @block.vector
        def _(dve):
            steps = [0]

            def step(ins):
                steps[0] += 1
                ins.then_inc(dve_step, 1)
                return steps[0]

            dve.sem_inc(sm_free, 2)
            dve.sem_inc(o_done, 1)
            dve.memset(xnT[:, 0:1], 0.0)
            step(dve.memset(v_all[:].rearrange("p (n e) -> p n e", e=VW)[:, :, HD:VW], 1.0))

            def vectors():
                dve.wait_ge(rows_loaded, 8 * 16)
                pair = rows[0:1, BQ:BK + 1, :].rearrange("p k (n two) -> p k n two", two=2)
                swap = rows[0:1, BQ_SWAP:BK_SWAP + 1, :].rearrange("p k (n two) -> p k n two", two=2)
                dve.tensor_copy(swap[:, :, :, 0], pair[:, :, :, 1])
                dve.tensor_copy(swap[:, :, :, 1], pair[:, :, :, 0]).then_inc(rows_done, 1)
                dve.wait_ge(vectors_spread, 1)
                dve.tensor_copy(bcast[:].rearrange("p k n -> p (k n)"), swap_bank(1)[:, 0:3 * P])
                done = step(dve.tensor_copy(cols[:], out_bank(0)[:, 0:N_COLS]))
                dve.wait_ge(dve_step, done)
                dve.tensor_scalar(omu[:], cols[:, MU_R:MU_K + 1], -1.0, 1.0, ALU.mult, ALU.add).then_inc(vectors_done, 1)

            def layer_norm(layer):
                for n in range(TILES):
                    if n % TPC == 0:
                        if layer == 0:
                            dve.wait_ge(x_loaded, 16 * CHUNKS)
                        else:
                            dve.wait_ge(x_new, CHUNKS * (layer - 1) + n // TPC + 1)
                    done = step(dve.bn_stats(stats[:, n, :], x[:, n, :]))
                dve.wait_ge(dve_step, done)
                for n in range(TILES):
                    done = step(dve.bn_aggr(mv[:, n, :], stats[:, n, :]))
                dve.wait_ge(dve_step, done)
                dve.tensor_scalar(veps[:], mv[:, :, 1], EPS, None, ALU.add).then_inc(var_ready, 1)
                dve.wait_ge(std_ready, layer + 1)
                done = step(dve.reciprocal(rstd[:], std[:]))
                dve.wait_ge(dve_step, done)
                for n in range(TILES):
                    last = dve.tensor_scalar(xn[:, n, :], x[:, n, :], mv[:, n, 0:1], rstd[:, n:n + 1],
                                             ALU.subtract, ALU.mult)
                    if n % TPC == TPC - 1:
                        last.then_inc(xn_ready, 1)

            def projections():
                col = (BK, BQ)

                def combine(n):
                    c, kq = n // 2, n % 2
                    cs = slice(c * CHUNK, (c + 1) * CHUNK)
                    dve.wait_ge(proj_ready, n + 1)
                    bias = cols[:, col[kq]:col[kq] + 1]
                    if n >= 1:
                        dve.wait_ge(comb_ready, n)
                    dve.scalar_tensor_tensor(out=rope1, in0=proj_bank(n), scalar=bias, in1=cos[:, cs],
                                             op0=ALU.add, op1=ALU.mult)
                    done = step(dve.scalar_tensor_tensor(
                        out=rope2, in0=swap_bank(n), scalar=cols[:, col[kq] + 2:col[kq] + 3],
                        in1=sin[:, cs], op0=ALU.add, op1=ALU.mult))
                    dve.wait_ge(dve_step, done)
                    if n >= 2:
                        dve.wait_ge(resid_ready, n - 1)
                        dve.wait_ge(hi_ready, n - 1)
                    dve.tensor_tensor(comb[:, n % 2, :], rope1, rope2, ALU.add).then_inc(comb_ready, 1)

                def residual(n):
                    c, kq = n // 2, n % 2
                    dve.wait_ge(hi_ready, n + 1)
                    if n >= 2:
                        dve.wait_ge(lo_ready, n - 1)
                        dve.wait_ge(mid_ready, n - 1)
                    dve.tensor_tensor(resid[:, n % 2, :], comb[:, n % 2, :],
                                      parts[kq][:, 0, c * CHUNK:(c + 1) * CHUNK], ALU.subtract).then_inc(resid_ready, 1)

                def low(n):
                    c, kq = n // 2, n % 2
                    dve.wait_ge(mid_ready, n + 1)
                    dve.tensor_tensor(parts[kq][:, 2, c * CHUNK:(c + 1) * CHUNK], resid[:, n % 2, :],
                                      parts[kq][:, 1, c * CHUNK:(c + 1) * CHUNK], ALU.subtract).then_inc(lo_ready, 1)

                dve.wait_ge(trig_loaded, 32)
                for n in range(2 * CHUNKS + 2):
                    if n < 2 * CHUNKS:
                        combine(n)
                    if 1 <= n <= 2 * CHUNKS:
                        residual(n - 1)
                    if n >= 2:
                        low(n - 2)
                    if n % 2 == 1 and n < 2 * CHUNKS:
                        c = n // 2
                        dve.wait_ge(v_ready, c + 1)
                        v_dst = v_all[:].rearrange("p (g t j e) -> p t g j e", g=GROUPS, t=TILES, j=HG)
                        for i in range(TPC):
                            last = dve.tensor_tensor(
                                v_dst[:, TPC * c + i, :, :, 0:HD],
                                out_bank(c)[:, i * P:(i + 1) * P].rearrange("p (g j d) -> p g j d", g=GROUPS, j=HG),
                                bcast[:, 0, :].rearrange("p (g j d) -> p g j d", g=GROUPS, j=HG), ALU.add)
                        last.then_inc(v_used, 1)

            def take_max(unit, r, kc):
                dve.wait_ge(sm_ready, unit * ROWS * KC + (KC * r + kc + 1))
                if r == 0 and kc == 0 and not (isinstance(unit, int) and unit == 0):
                    dve.wait_ge(max_step, unit * MSTEPS - (MSTEPS - 1))
                dve.tensor_reduce(mpart[:, KC * r + kc:KC * r + kc + 1], sm_bank(kc), AX_X,
                                  ALU.max).then_inc(sm_free, 1)

            def max_parts(unit, i):
                def wait_step(k):
                    dve.wait_ge(max_step, unit * MSTEPS + k)

                if i == 0:
                    dve.wait_ge(sm_free, unit * ROWS * KC + (ROWS * KC + 2))
                    dve.tensor_reduce(nmax[:], mpart[:].rearrange("p (r k) -> p r k", k=KC), AX_X, ALU.max,
                                      negate=True).then_inc(max_step, 1)
                if i == 1:
                    wait_step(1)
                    dve.tensor_copy(nmax_p[:, :, 0], nmax[:]).then_inc(max_step, 1)
                if i == 2:
                    wait_step(2)
                    dve.tensor_tensor(nmax_r[:, 0, :], nmax[:], nmax_p[:, :, 0], ALU.subtract).then_inc(max_step, 1)
                if i == 3:
                    wait_step(3)
                    dve.tensor_copy(nmax_p[:, :, 1], nmax_r[:, 0, :]).then_inc(max_step, 1)
                if i == 4:
                    wait_step(4)
                    dve.tensor_tensor(nmax_r[:, 1, :], nmax_r[:, 0, :], nmax_p[:, :, 1],
                                      ALU.subtract).then_inc(max_step, 1)
                if i == 5:
                    wait_step(5)
                    dve.tensor_copy(nmax_p[:, :, 2], nmax_r[:, 1, :]).then_inc(max_step, 1)

            def norm_recip(unit):
                dve.wait_ge(o_turned, unit + 1)
                dve.reciprocal(rden[:].rearrange("p (q j e) -> p q j e", q=TPC, e=1),
                               misc_o[:, :, :, HD:VW]).then_inc(rden_ready, 1)

            def norm_mul(unit):
                dve.wait_ge(rden_ready, unit + 1)
                dve.tensor_tensor(
                    attn[:, bass.ds((unit % CHUNKS) * TPC, TPC), bass.ds((unit // CHUNKS) * (HG * HD), HG * HD)
                         ].rearrange("p q (j d) -> p q j d", j=HG),
                    misc_o[:, :, :, 0:HD],
                    rden[:].rearrange("p (q j e) -> p q j e", q=TPC, e=1).to_broadcast([P, TPC, HG, HD]),
                    ALU.mult).then_inc(o_done, 1)

            def unit_body(unit, has_next, has_second, has_before):
                for t in range(STEPS):
                    there = has_next if t < STEPS - LEAD else has_second
                    for kc in range(KC):
                        if there:
                            v, r = max_row(unit, t)
                            take_max(v, r, kc)
                        if has_before and t == 2 and kc == 2:
                            norm_recip(unit - 1)
                        if has_before and t == 2 and kc == 3:
                            norm_mul(unit - 1)
                        k = (t - (STEPS - LEAD)) * KC + kc + 1
                        if has_next and 0 <= k < MSTEPS:
                            max_parts(unit + 1, k)

            def attention():
                for r in range(ROWS):
                    for kc in range(KC):
                        take_max(0, r, kc)
                for i in range(MSTEPS):
                    max_parts(0, i)
                for r in range(LEAD):
                    for kc in range(KC):
                        take_max(1, r, kc)
                attention_units(dve, unit_body)
                norm_recip(UNITS - 1)
                norm_mul(UNITS - 1)

            def head_attention():
                head = qkv[:].rearrange("p n (h e) -> p n h e", h=H)
                shape = [P, H, H, HD]
                done = {}

                def products(i, kind, n):
                    buf = i % 3
                    if i >= 3:
                        dve.wait_ge(dve_step, done["sum", i - 3])
                    if kind == "qk":
                        dve.wait_ge(qkv_copied, n + 1)
                        q = head[:, n, :, 0:HD].unsqueeze(2).to_broadcast(shape)
                        k = head[:, n, :, HD:2 * HD].unsqueeze(1).to_broadcast(shape)
                        dst = prod[:, buf, :].rearrange("p (h g d) -> p h g d", h=H, g=H)
                    else:
                        if n % TPC == 0:
                            dve.wait_ge(he_ready, n // TPC + 1)
                        q = he[:, n, :].rearrange("p (h g) -> p h g", h=H).unsqueeze(2).to_broadcast([P, H, HD, H])
                        k = head[:, n, :, 2 * HD:3 * HD].rearrange("p g d -> p d g").unsqueeze(1).to_broadcast(
                            [P, H, HD, H])
                        dst = prod[:, buf, :].rearrange("p (h d g) -> p h d g", h=H, d=HD)
                    done["product", i] = step(dve.tensor_tensor(dst, q, k, ALU.mult))

                def sums(i, kind, n):
                    dve.wait_ge(dve_step, done["product", i])
                    if kind == "qk":
                        done["sum", i] = step(dve.tensor_reduce(
                            hs[:, n, :], prod[:, i % 3, :].rearrange("p (s d) -> p s d", d=HD), AX_X, ALU.add))
                    else:
                        done["sum", i] = step(dve.tensor_reduce(
                            ctx_raw[:, n, :], prod[:, i % 3, :].rearrange("p (s g) -> p s g", g=H), AX_X, ALU.add))

                def after(i, kind, n):
                    if n % TPC != TPC - 1:
                        return
                    c = n // TPC
                    tiles = slice(c * TPC, (c + 1) * TPC)
                    if kind == "qk":
                        dve.wait_ge(dve_step, done["sum", i])
                        sc = hs[:, tiles, :].rearrange("p n (h g) -> p (n h) g", h=H)
                        got = step(dve.tensor_reduce(hmax[:], sc, AX_X, ALU.max))
                        dve.wait_ge(dve_step, got)
                        dve.tensor_tensor(sc, sc, hmax[:].unsqueeze(2).to_broadcast([P, TPC * H, H]),
                                          ALU.subtract).then_inc(hs_ready, 1)
                        dve.wait_ge(hs_ready, c + 1)
                    else:
                        got = step(dve.tensor_reduce(hden[:], he[:, tiles, :].rearrange(
                            "p n (h g) -> p (n h) g", h=H), AX_X, ALU.add))
                        dve.wait_ge(dve_step, got)
                        got = step(dve.reciprocal(hrden[:], hden[:]))
                        dve.wait_ge(dve_step, got)
                        got = step(dve.tensor_tensor(
                            attn[:, tiles, :].rearrange("p n (h d) -> p (n h) d", h=H),
                            ctx_raw[:, tiles, :].rearrange("p n (h d) -> p (n h) d", h=H),
                            hrden[:].unsqueeze(2).to_broadcast([P, TPC * H, HD]), ALU.mult))
                        dve.wait_ge(dve_step, got)
                        dve.sem_inc(ctx_ready, 1)

                items = []
                for c in range(CHUNKS + 1):
                    if c < CHUNKS:
                        items += [("qk", TPC * c + i) for i in range(TPC)]
                    if c >= 1:
                        items += [("pv", TPC * (c - 1) + i) for i in range(TPC)]
                for i in range(len(items) + 1):
                    if i < len(items):
                        products(i, *items[i])
                    if i >= 1:
                        sums(i - 1, *items[i - 1])
                        after(i - 1, *items[i - 1])

            def output_projection(a):
                dve.wait_ge(xb_ready, a + 1)
                for c in range(CHUNKS):
                    dve.wait_ge(op_ready, CHUNKS * a + c + 1)
                    xc = x[:, c * TPC:(c + 1) * TPC, :].rearrange("p n d -> p (n d)")
                    dve.tensor_tensor(xc, out_bank(c), xc, ALU.add).then_inc(x_new, 1)

            def ffn(a):
                layer = 2 * a + 1

                def mixes(c):
                    dve.wait_ge(turned_copied, CHUNKS * (3 * a + 2) + c + 1)
                    if c >= 2:
                        dve.wait_ge(rk_ready, CHUNKS * a + c - 1)
                    cur = xnT[:, 1 + c * CHUNK:1 + (c + 1) * CHUNK]
                    prev = xnT[:, c * CHUNK:(c + 1) * CHUNK]
                    dve.tensor_scalar(ffn_r[:, c % 2, :], cur, cols[:, MU_R:MU_R + 1], None, ALU.mult)
                    done = step(dve.tensor_scalar(ffn_k[:, c % 2, :], cur, cols[:, MU_K:MU_K + 1], None, ALU.mult))
                    dve.wait_ge(dve_step, done)
                    dve.scalar_tensor_tensor(out=ffn_r[:, c % 2, :], in0=prev, scalar=omu[:, 0:1],
                                             in1=ffn_r[:, c % 2, :], op0=ALU.mult, op1=ALU.add)
                    dve.scalar_tensor_tensor(out=ffn_k[:, c % 2, :], in0=prev, scalar=omu[:, 1:2],
                                             in1=ffn_k[:, c % 2, :], op0=ALU.mult, op1=ALU.add).then_inc(mixed, 1)

                def gated(c):
                    dve.wait_ge(kv_ready, CHUNKS * a + c + 1)
                    dve.wait_ge(gate_ready, CHUNKS * a + c + 1)
                    done = step(dve.tensor_tensor(gate[:, c % 2, :], out_bank(c), gate[:, c % 2, :], ALU.mult))
                    dve.wait_ge(dve_step, done)
                    xc = x[:, c * TPC:(c + 1) * TPC, :].rearrange("p n d -> p (n d)")
                    dve.tensor_tensor(xc, gate[:, c % 2, :], xc, ALU.add).then_inc(x_new, 1)

                for c in range(CHUNKS + 1):
                    if c < CHUNKS:
                        mixes(c)
                    if c >= 1:
                        gated(c - 1)

            layer_norm(0)
            vectors()
            projections()
            attention()
            output_projection(0)
            layer_norm(1)
            ffn(0)
            layer_norm(2)
            head_attention()
            output_projection(1)
            layer_norm(3)
            ffn(1)

        @block.tensor
        def _(pe):
            pe.sem_inc(pv_done, RING)
            pe.wait_ge(ident_ready, 1)

            def setup():
                pe.wait_ge(w_loaded, 9 * 16)
                for i in range(3):
                    last = pe.transpose(out_bank(1)[:, i * P:(i + 1) * P], wf_in[:, i, :], ident[:])
                last.then_inc(weights_turned, 1)
                pe.wait_ge(rows_done, 1)
                for i in range(N_COLS):
                    pe.matmul(out_bank(0)[:, i:i + 1], rows[0:1, i, :], ones_row[0:1, 0:1], start=True, stop=True)
                for i in range(3):
                    last = pe.matmul(swap_bank(1)[:, i * P:(i + 1) * P], ones_row[:], rows[0:1, N_COLS + i, :],
                                     start=True, stop=True)
                last.then_inc(vectors_spread, 1)

            def turn(tile_of, n, c):
                if c >= 2:
                    pe.wait_ge(turned_copied, n - 1)
                for i in range(TPC):
                    last = pe.transpose(turn_bank(c)[:, i * P:(i + 1) * P], tile_of(TPC * c + i), ident[:])
                last.then_inc(turned, 1)

            def layer_norm(layer):
                for c in range(CHUNKS):
                    pe.wait_ge(xn_ready, CHUNKS * layer + c + 1)
                    turn(lambda i: xn[:, i, :], CHUNKS * (layer + (layer + 1) // 2) + c, c)

            def projections():
                w = (wa[:, 1, :], wa[:, 0, :])
                w_v = wa[:, 2, :]
                pe.wait_ge(weights_done, 1)
                pe.wait_ge(vectors_done, 1)
                for c in range(CHUNKS):
                    pe.wait_ge(turned_copied, c + 1)
                    xc = xnT[:, 1 + c * CHUNK:1 + (c + 1) * CHUNK]
                    for kq in range(2):
                        n = 2 * c + kq
                        if n >= 2:
                            pe.wait_ge(comb_ready, n - 1)
                        pe.matmul(proj_bank(n), w[kq], xc, start=True, stop=True)
                        pe.matmul(swap_bank(n), wsw[:, 1 - kq, :], xc, start=True,
                                  stop=True).then_inc(proj_ready, 1)
                    if c >= 2:
                        pe.wait_ge(v_used, c - 1)
                    for i in range(TPC):
                        last = pe.matmul(out_bank(c)[:, i * P:(i + 1) * P], xc[:, i * P:(i + 1) * P], w_v,
                                         start=True, stop=True)
                    last.then_inc(v_ready, 1)

            def max_scores(unit, r, kc):
                j, qt = r // TPC, r % TPC
                pe.wait_ge(sm_free, unit * ROWS * KC + (KC * r + kc + 1))
                pe.matmul(sm_bank(kc), q_cols(unit, j, qt * P, P), k_cols(unit, j, kc * CHUNK, CHUNK),
                          start=True, stop=True).then_inc(sm_ready, 1)

            def scores(unit, t, pair):
                pe.wait_ge(exp_done, unit * 2 * STEPS + (2 * t + pair + 1))
                for jj in range(2):
                    j = 2 * pair + jj
                    last = pe.matmul(st_bank(pair, jj), k_cols(unit, j, t * P, P), q_cols(unit, j, 0, CHUNK),
                                     start=True, stop=True)
                last.then_inc(st_ready, 1)

            def product_v(unit, t):
                if t == 0:
                    pe.wait_ge(v_unit_ready, unit + 1)
                pe.wait_ge(exp_done, unit * 2 * STEPS + (2 * t + 2 + 2))
                for j in range(HG):
                    last = pe.matmul(acc[STRIP * j:STRIP * (j + 1), :], v_unit[:, t, j, :],
                                     probs[:, t % RING, j * CHUNK:(j + 1) * CHUNK],
                                     start=(t == 0), stop=(t == STEPS - 1))
                last.then_inc(pv_done, 1)

            def turn_output(unit):
                pe.wait_ge(o_copied, unit + 1)
                pe.wait_ge(o_done, unit + 1)
                for q in range(TPC):
                    last = pe.transpose(misc[:, q * P:(q + 1) * P], o_unit[:, q * P:(q + 1) * P], ident[:])
                last.then_inc(o_turned, 1)

            def turn_max(unit, half):
                if half == 0:
                    pe.wait_ge(max_step, unit * MSTEPS + MSTEPS)
                    pe.wait_ge(o_done, 1 if isinstance(unit, int) and unit < 2 else unit)
                else:
                    pe.wait_ge(max_copied, unit * 2 + 1)
                for i in range(ROWS // 2):
                    last = pe.transpose(misc_b[MROW:MROW + 3, i * P:(i + 1) * P],
                                        nmax_p[:, half * (ROWS // 2) + i, :], ident_b[:])
                last.then_inc(max_turned, 1)

            def unit_body(unit, has_next, has_second, has_before):
                pe.wait_ge(max_copied, unit * 2 + 2)
                for t in range(STEPS):
                    there = has_next if t < STEPS - LEAD else has_second
                    v, r = max_row(unit, t)
                    last_step = t == STEPS - 1
                    if t == STEPS - LEAD and has_second:
                        pe.wait_ge(stacks_ready, (unit + 2) // CHUNKS + 1)
                    scores(unit, t, 0)
                    if there:
                        max_scores(v, r, 0)
                    if last_step:
                        product_v(unit, t - LAG)
                    elif there:
                        max_scores(v, r, 1)
                    scores(unit, t, 1)
                    if last_step:
                        if there:
                            max_scores(v, r, 1)
                        product_v(unit, t - 1)
                    if there:
                        max_scores(v, r, 2)
                        max_scores(v, r, 3)
                    if t == 2 and has_before:
                        turn_output(unit - 1)
                    if has_next and t in (STEPS - 3, STEPS - 2):
                        turn_max(unit + 1, t - (STEPS - 3))
                    if last_step:
                        product_v(unit, t)
                    elif t >= LAG:
                        product_v(unit, t - LAG)

            def attention():
                pe.wait_ge(stacks_ready, 1)
                for r in range(ROWS):
                    for kc in range(KC):
                        max_scores(0, r, kc)
                for r in range(LEAD):
                    for kc in range(KC):
                        max_scores(1, r, kc)
                    if r == 1:
                        turn_max(0, 0)
                turn_max(0, 1)
                attention_units(pe, unit_body)
                turn_output(UNITS - 1)

            def head_qkv():
                for n in range(TILES):
                    pe.wait_ge(turned_copied, 3 * CHUNKS + n // TPC + 1)
                    if n >= 4:
                        pe.wait_ge(qkv_copied, n - 3)
                    first = 1 + n * P
                    pe.matmul(qkv_bank(n), xnT[:, first:first + P], wqkv[:], start=True, stop=False)
                    pe.matmul(qkv_bank(n), ones_row[:], rows[0:1, B_QKV:N_ROWS, :].rearrange("p k d -> p (k d)"),
                              start=False, stop=True).then_inc(qkv_ready, 1)

            def output_projection(a):
                if a == 0:
                    pe.wait_ge(o_done, UNITS + 1)
                for c in range(CHUNKS):
                    if a == 1:
                        pe.wait_ge(ctx_ready, c + 1)
                    turn(lambda i: attn[:, i, :], CHUNKS * (3 * a + 1) + c, c)
                for c in range(CHUNKS):
                    pe.wait_ge(turned_copied, CHUNKS * (3 * a + 1) + c + 1)
                    if c >= 2:
                        pe.wait_ge(x_new, CHUNKS * 2 * a + c - 1)
                    for i in range(TPC):
                        first = 1 + (TPC * c + i) * P
                        last = pe.matmul(out_bank(c)[:, i * P:(i + 1) * P], xnT[:, first:first + P],
                                         (wa[:, 3, :], wout[:])[a], start=True, stop=True)
                    last.then_inc(op_ready, 1)

            def ffn(a):
                def gates(c):
                    pe.wait_ge(mixed, CHUNKS * a + c + 1)
                    if c >= 2:
                        pe.wait_ge(relu_ready, CHUNKS * a + c - 1)
                    for i in range(TPC):
                        pe.matmul(proj_bank(c)[:, i * P:(i + 1) * P], ffn_r[:, c % 2, i * P:(i + 1) * P],
                                  wfT[:, 0, :], start=True, stop=True)
                    pe.matmul(swap_bank(c), wfT[:, 1, :], ffn_k[:, c % 2, :], start=True,
                              stop=True).then_inc(rk_ready, 1)

                def values(c):
                    pe.wait_ge(act_ready, CHUNKS * a + c + 1)
                    if c >= 2:
                        pe.wait_ge(x_new, CHUNKS * (2 * a + 1) + c - 1)
                    for i in range(TPC):
                        last = pe.matmul(out_bank(c)[:, i * P:(i + 1) * P], act2[:, c % 2, i * P:(i + 1) * P],
                                         wfT[:, 2, :], start=True, stop=True)
                    last.then_inc(kv_ready, 1)

                for c in range(CHUNKS + 1):
                    if c < CHUNKS:
                        gates(c)
                    if c >= 1:
                        values(c - 1)

            layer_norm(0)
            setup()
            projections()
            attention()
            output_projection(0)
            layer_norm(1)
            ffn(0)
            layer_norm(2)
            head_qkv()
            output_projection(1)
            layer_norm(3)
            ffn(1)


def rope_tables():
    inv_freq = (np.float32(1.0) / np.float32(ROPE_BASE) ** (np.arange(0, HD, 2, dtype=np.float32) / np.float32(HD)))
    freqs = np.arange(S, dtype=np.float32)[:, None] * inv_freq.astype(np.float32)
    cos = np.repeat(np.cos(freqs), 2, axis=-1).T
    sin = np.repeat(np.sin(freqs), 2, axis=-1).T
    sign = np.where(np.arange(HD) % 2 == 0, np.float32(-1.0), np.float32(1.0))[:, None]
    return (np.ascontiguousarray(np.tile(cos, (H, 1)).astype(np.float32)),
            np.ascontiguousarray(np.tile(sin * sign, (H, 1)).astype(np.float32)))


COS, SIN = rope_tables()
ZERO_ROWS = np.zeros((3, HG * S // 2), np.float32)

_INS = ['L0_attn_a_x', 'L0_attn_a_Wq', 'L0_attn_a_bq', 'L0_attn_a_Wk', 'L0_attn_a_bk', 'L0_attn_a_Wv',
        'L0_attn_a_bv', 'L0_attn_a_Wp', 'L0_attn_a_bp', 'L0_attn_b_W_qkv', 'L0_attn_b_b_qkv',
        'L0_attn_b_W_out', 'L0_attn_b_b_out', 'L0_ffn_W_r', 'L0_ffn_W_k', 'L0_ffn_W_v', 'L0_ffn_mu_r',
        'L0_ffn_mu_k']


def kernel(**inputs):
    import concourse.bacc as _bacc
    from concourse.bass_utils import run_bass_kernel_spmd as _run

    nc = _bacc.Bacc("TRN2", target_bir_lowering=False, num_devices=1)
    arrays, args = {}, []
    named = {n: np.ascontiguousarray(inputs[n]) for n in _INS}
    named['L0_attn_a_x'] = named['L0_attn_a_x'].reshape(S, P)
    named.update(rope_cos=COS, rope_sin=SIN, zero_rows=ZERO_ROWS)
    for name, a in named.items():
        arrays[f"in_{name}"] = a
        args.append(nc.dram_tensor(f"in_{name}", a.shape, mybir.dt.from_np(a.dtype), kind="ExternalInput").ap())
    args.append(nc.dram_tensor("out_x", (S, P), F32, kind="ExternalOutput").ap())
    build(nc, *args)
    r = _run(nc, [arrays], core_ids=[0])
    return r.results[0]["out_x"].reshape(1, S, P)
```

```python
from contextlib import ExitStack

import numpy as np

import concourse.bass as bass
from concourse import mybir

F32 = mybir.dt.float32
BF16 = mybir.dt.bfloat16
ALU = mybir.AluOpType
ACT = mybir.ActivationFunctionType
AX_X = mybir.AxisListType.X

P = 128
S = 2048
H, HD = 16, 8
TILES = S // P
CHUNK = 512
CHUNKS = S // CHUNK
TPC = CHUNK // P
HG = 4
GROUPS = H // HG
UNITS = GROUPS * CHUNKS
STEPS = TILES
ROWS = HG * TPC
KC = 2
KW = S // KC
LEAD = 4
LAG = 2
SLOTS = 3
MAX_STEPS = (STEPS - 3, STEPS - 2)
ITEMS = HG * STEPS + 2
TOTAL_ITEMS = UNITS * ITEMS
TURN_STEP = 3
RING = 4
VW = HD + 1
STRIP = 32
PARTS_Q = (0, 0, 1, 0, 2, 1)
PARTS_K = (0, 1, 0, 2, 0, 1)
MROW = 64
SCALE = float(1.0 / np.sqrt(HD))
EPS = 1e-5
ROPE_BASE = 10000.0

(BQ, BK, BQ_SWAP, BK_SWAP, MU_R, MU_K, BV, BP, B_OUT, B_QKV) = range(10)
N_COLS = 6
N_ROWS = 12


def build(nc, x_in, wq, bq, wk, bk, wv, bv, wp, bp, w_qkv, b_qkv, w_out, b_out,
          w_r, w_k, w_v, mu_r, mu_k, cos_t, sin_t, zero_rows, out):
    with ExitStack() as ctx:
        def sb(name, shape, dt):
            return ctx.enter_context(nc.sbuf_tensor(name, shape, dt))

        def sem(name):
            return ctx.enter_context(nc.semaphore(name))

        psum = ctx.enter_context(nc.psum_tensor("psum", [P, 8, CHUNK], F32))

        x = sb("x", [P, TILES, P], F32)
        xnT = sb("xnT", [P, 1 + S], F32)
        attn = sb("attn", [P, TILES, P], F32)
        xn = attn
        kst = sb("kst", [P, 2 * HG * S], BF16)
        qst = sb("qst", [P, 2, HG, CHUNKS, CHUNK], BF16)
        qflat = qst[:].rearrange("p a j c t -> p (a j c t)")
        probs = sb("probs", [P, RING, HG * CHUNK], F32)
        v_all = sb("v_all", [P, GROUPS * TILES * HG * VW], F32)
        v_unit = sb("v_unit", [P, TILES, HG, STRIP], F32)
        o_unit = sb("o_unit", [P, CHUNK], F32)
        parts = [sb("k_parts", [P, 3, S], BF16), sb("q_parts", [P, 3, S], BF16)]

        def in_probs(slot, half):
            return probs[:, slot, half * 2 * CHUNK:(half + 1) * 2 * CHUNK].rearrange("p (b t) -> p b t", b=2)

        cos = probs[:, 0, :]
        sin = probs[:, 1, :]
        comb = in_probs(2, 0)
        rope1 = in_probs(2, 1)[:, 0, :]
        rope2 = in_probs(2, 1)[:, 1, :]
        resid = in_probs(3, 0)
        ffn_r = in_probs(0, 0)
        ffn_k = in_probs(0, 1)
        gate = in_probs(1, 0)
        relu = in_probs(1, 1)
        act2 = in_probs(2, 0)
        qkv = kst[:].bitcast(F32)[:, 0:TILES * 3 * P].rearrange("p (n e) -> p n e", n=TILES)
        prod = probs[:, 0:3, :]
        hs = qflat.bitcast(F32)[:, 0:TILES * H * H].rearrange("p (n e) -> p n e", n=TILES)
        he = qflat.bitcast(F32)[:, TILES * H * H:2 * TILES * H * H].rearrange("p (n e) -> p n e", n=TILES)
        ctx_raw = probs[:, 3, 0:CHUNK].rearrange("p (n e) -> p n e", n=TPC)
        hmax = sb("hmax", [P, TPC * H], F32)
        hden = sb("hden", [P, TPC * H], F32)
        hrden = sb("hrden", [P, TPC * H], F32)
        wa = sb("wa", [P, 4, P], F32)
        wsw = sb("wsw", [P, 2, P], F32)
        wqkv = sb("wqkv", [P, 3 * P], F32)
        wout = sb("wout", [P, P], F32)
        wf_in = sb("wf_in", [P, 3, P], F32)
        wfT = sb("wfT", [P, 3, P], F32)
        rows = sb("rows", [1, N_ROWS, P], F32)
        cols = sb("cols", [P, N_COLS], F32)
        omu = sb("omu", [P, 2], F32)
        bcast = sb("bcast", [P, 3, P], F32)
        ident = sb("ident", [P, P], F32)
        ident_b = sb("ident_b", [P, P], BF16)
        ones_row = sb("ones_row", [1, P], F32)
        stats = sb("stats", [P, TILES, 6], F32)
        mv = sb("mv", [P, TILES, 2], F32)
        veps = sb("veps", [P, TILES], F32)
        std = sb("std", [P, TILES], F32)
        rstd = sb("rstd", [P, TILES], F32)
        mpart = sb("mpart", [P, ROWS * KC], F32)
        nmax = sb("nmax", [P, ROWS], F32)
        nmax_r = sb("nmax_r", [P, 2, ROWS], F32)
        nmax_p = sb("nmax_p", [P, ROWS, 3], BF16)
        o_tok = sb("o_tok", [P, TPC * HG, VW], F32)
        rden = sb("rden", [P, TPC * HG], F32)

        scratch = [nc.dram_tensor("k_scratch", (3, P, S), BF16, kind="Internal").ap(),
                   nc.dram_tensor("q_scratch", (3, P, S), BF16, kind="Internal").ap()]

        x_loaded = sem("x_loaded")
        w_loaded = sem("w_loaded")
        rows_loaded = sem("rows_loaded")
        trig_loaded = sem("trig_loaded")
        pool_step = sem("pool_step")
        ident_ready = sem("ident_ready")
        zeroed = sem("zeroed")
        rows_done = sem("rows_done")
        weights_turned = sem("weights_turned")
        vectors_spread = sem("vectors_spread")
        weights_done = sem("weights_done")
        vectors_done = sem("vectors_done")
        dve_step = sem("dve_step")
        var_ready = sem("var_ready")
        std_ready = sem("std_ready")
        xn_ready = sem("xn_ready")
        turned = sem("turned")
        turned_copied = sem("turned_copied")
        proj_ready = sem("proj_ready")
        comb_ready = sem("comb_ready")
        hi_ready = sem("hi_ready")
        resid_ready = sem("resid_ready")
        mid_ready = sem("mid_ready")
        lo_ready = sem("lo_ready")
        v_ready = sem("v_ready")
        v_used = sem("v_used")
        scratch_written = sem("scratch_written")
        stack_loading = sem("stack_loading")
        stacks_ready = sem("stacks_ready")
        sm_ready = sem("sm_ready")
        sm_free = sem("sm_free")
        ring_ready = sem("ring_ready")
        ring_taken = sem("ring_taken")
        pv_done = sem("pv_done")
        v_unit_ready = sem("v_unit_ready")
        o_copied = sem("o_copied")
        o_turned = sem("o_turned")
        o_taken = sem("o_taken")
        rden_ready = sem("rden_ready")
        o_done = sem("o_done")
        max_step = sem("max_step")
        qkv_ready = sem("qkv_ready")
        qkv_copied = sem("qkv_copied")
        prod_ready = sem("prod_ready")
        pe_summed = sem("pe_summed")
        dve_summed = sem("dve_summed")
        hs_ready = sem("hs_ready")
        he_ready = sem("he_ready")
        ctx_ready = sem("ctx_ready")
        xb_ready = sem("xb_ready")
        op_ready = sem("op_ready")
        x_new = sem("x_new")
        mixed = sem("mixed")
        rk_ready = sem("rk_ready")
        gate_ready = sem("gate_ready")
        relu_ready = sem("relu_ready")
        act_ready = sem("act_ready")
        kv_ready = sem("kv_ready")
        stored = sem("stored")

        MSTEPS = 6

        def turn_bank(c):
            return psum[:, c % 2, :]

        def proj_bank(n):
            return psum[:, 2 + n % 2, :]

        def swap_bank(n):
            return psum[:, 4 + n % 2, :]

        def out_bank(c):
            return psum[:, 6 + c % 2, :]

        def qkv_bank(n):
            return psum[:, 2 + n % 4, 0:3 * P]

        def hs_banks(c):
            return psum[:, 2 + 2 * (c % 2):4 + 2 * (c % 2), :].rearrange("p b t -> p (b t)")

        items = []
        for c in range(CHUNKS + 1):
            if c < CHUNKS:
                items += [("qk", TPC * c + i) for i in range(TPC)]
            if c >= 1:
                items += [("pv", TPC * (c - 1) + i) for i in range(TPC)]

        def summed_by_dve(kind, n):
            return kind == "pv" and n // TPC == CHUNKS - 1

        def item(unit, t, j):
            more = sum(t > m for m in MAX_STEPS) if has_next_unit(unit) else 0
            return unit * ITEMS + (2 + HG * t + j + more)

        def has_next_unit(unit):
            return not (isinstance(unit, int) and unit == UNITS - 1)

        def max_item(unit, half):
            if isinstance(unit, int) and unit == 0:
                return half
            return unit * ITEMS + (2 + HG * (MAX_STEPS[half] + 1) + half - ITEMS)

        def slot(unit, t, j):
            return item(0 if has_next_unit(unit) else UNITS - 1, t, j) % SLOTS

        def sm_banks(kc):
            return psum[:, SLOTS + 2 * kc:SLOTS + 2 + 2 * kc, :].rearrange("p b t -> p (b t)")

        acc = psum[:, 7, :]

        def max_rows(bank):
            return psum[MROW:MROW + 3, bank, :].bitcast(BF16)

        def max_slot(unit, half):
            first = isinstance(unit, int) and unit == 0
            return (half if first else item(0, MAX_STEPS[half], HG - 1) + 1) % SLOTS

        def turned_slot(last):
            return ((TOTAL_ITEMS if last else item(0, TURN_STEP, HG - 1)) + 1) % SLOTS

        def k_cols(unit, j, first, n):
            return kst[:, bass.ds(((unit // CHUNKS) % 2) * (HG * S) + (j * S + first), n)]

        def q_cols(unit, j, first, n):
            return qflat[:, bass.ds(((unit // CHUNKS) % 2) * (HG * S) + (unit % CHUNKS) * CHUNK + (j * S + first), n)]

        def max_row(unit, t):
            return (unit + 1, t + LEAD) if t < STEPS - LEAD else (unit + 2, t + LEAD - STEPS)

        def attention_units(eng, body):
            body(0, True, True, False)
            with eng.Fori(1, UNITS - 2) as unit:
                body(unit, True, True, True)
            body(UNITS - 2, True, False, True)
            body(UNITS - 1, False, False, True)

        block = ctx.enter_context(nc.Block())

        @block.sync
        def _(sp):
            for c in range(CHUNKS):
                src = x_in[c * CHUNK:(c + 1) * CHUNK, :].rearrange("(n p) d -> p n d", p=P)
                sp.dma_start(x[:, c * TPC:(c + 1) * TPC, :], src).then_inc(x_loaded, 16)
            for i, w in enumerate((wq, wk, wv, wp)):
                sp.dma_start(wa[:, i, :], w).then_inc(w_loaded, 16)
            sp.dma_start(wqkv[:], w_qkv).then_inc(w_loaded, 16)
            sp.dma_start(wout[:], w_out).then_inc(w_loaded, 16)
            for i, w in enumerate((w_r, w_k, w_v)):
                sp.dma_start(wf_in[:, i, :], w).then_inc(w_loaded, 16)
            sp.dma_start(cos, cos_t).then_inc(trig_loaded, 16)
            sp.dma_start(sin, sin_t).then_inc(trig_loaded, 16)

            for n in range(2 * CHUNKS):
                c, kq = n // 2, n % 2
                sp.wait_ge(lo_ready, n + 1)
                cs = slice(c * CHUNK, (c + 1) * CHUNK)
                sp.dma_start(scratch[kq][:, :, cs].rearrange("s p t -> p s t"),
                             parts[kq][:, :, cs]).then_inc(scratch_written, 16)
            sp.wait_ge(scratch_written, 2 * CHUNKS * 16)
            sp.wait_ge(zeroed, 1)
            for g in range(GROUPS):
                half = g % 2
                if g >= 2:
                    sp.wait_ge(ring_taken, SLOTS + item((g - 1) * CHUNKS, 0, 0))
                heads = slice(g * HG * HD, (g + 1) * HG * HD)
                kdst = kst[:].rearrange("p (a j t) -> p a j t", a=2, j=HG)
                for slot in range(len(PARTS_K)):
                    at = slice(HD * slot, HD * slot + HD)
                    sp.dma_start(kdst[at, half], scratch[0][PARTS_K[slot], heads, :].rearrange(
                        "(j d) t -> d j t", j=HG)).then_inc(stack_loading, 16)
                    sp.dma_start(qst[at, half].rearrange("p j c t -> p j (c t)"),
                                 scratch[1][PARTS_Q[slot], heads, :].rearrange(
                                     "(j d) t -> d j t", j=HG)).then_inc(stack_loading, 16)
                sp.dma_start(qst[MROW:MROW + 3, half].rearrange("p j c t -> p (j c t)").bitcast(F32),
                             zero_rows).then_inc(stack_loading, 16)
                sp.wait_ge(stack_loading, 13 * 16 * (g + 1))
                sp.sem_inc(stacks_ready, 1)
            for c in range(CHUNKS):
                sp.wait_ge(x_new, 3 * CHUNKS + c + 1)
                dst = out[c * CHUNK:(c + 1) * CHUNK, :].rearrange("(n p) d -> p n d", p=P)
                sp.dma_start(dst, x[:, c * TPC:(c + 1) * TPC, :]).then_inc(stored, 16)
            sp.wait_ge(stored, 16 * CHUNKS)

        @block.gpsimd
        def _(pool):
            def row(slot, src):
                pool.dma_start(rows[0:1, slot, :], src).then_inc(rows_loaded, 16)

            for slot, v in ((BQ, bq), (BK, bk), (BV, bv), (BP, bp), (B_OUT, b_out), (MU_R, mu_r), (MU_K, mu_k)):
                row(slot, v.rearrange("(a d) -> a d", a=1))
            pool.dma_start(rows[0:1, B_QKV:N_ROWS, :].rearrange("p k d -> p (k d)"),
                           b_qkv.rearrange("(a d) -> a d", a=1)).then_inc(rows_loaded, 16)
            pool.memset(ident[:], 0.0).then_inc(pool_step, 1)
            pool.memset(ones_row[:], 1.0).then_inc(pool_step, 1)
            pool.wait_ge(pool_step, 2)
            pool.affine_select(out=ident[:], in_=ident[:], compare_op=ALU.not_equal, fill=1.0, base=0,
                               pattern=[[-1, P]], channel_multiplier=1).then_inc(pool_step, 1)
            pool.wait_ge(pool_step, 3)
            pool.tensor_copy(ident_b[:], ident[:]).then_inc(ident_ready, 1)
            pool.memset(kst[:].bitcast(F32), 0.0).then_inc(pool_step, 1)
            pool.memset(qflat.bitcast(F32), 0.0).then_inc(pool_step, 1)
            pool.memset(v_unit[:], 0.0).then_inc(pool_step, 1)
            pool.wait_ge(pool_step, 6)
            pool.memset(kst[MROW:MROW + 3, :], 1.0).then_inc(zeroed, 1)
            pool.wait_ge(zeroed, 1)
            pool.wait_ge(vectors_done, 1)
            pool.wait_ge(xn_ready, CHUNKS)
            pool.tensor_tensor(x[:], x[:], bcast[:, 1, :].unsqueeze(1).to_broadcast([P, TILES, P]),
                               ALU.add).then_inc(xb_ready, 1)
            pool.wait_ge(v_used, CHUNKS)
            with pool.Fori(0, UNITS) as unit:
                for first, n in ((0, TILES - LAG), (TILES - LAG, LAG)):
                    pool.wait_ge(pv_done, unit * STEPS + (RING + first + n - STEPS))
                    pool.tensor_copy(
                        v_unit[:, first:first + n, :, 0:VW],
                        v_all[:, bass.ds((unit // CHUNKS) * (TILES * HG * VW) + first * HG * VW, n * HG * VW)
                              ].rearrange("p (t j e) -> p t j e", t=n, j=HG)).then_inc(v_unit_ready, 1)
            pool.wait_ge(xn_ready, 3 * CHUNKS)
            pool.tensor_tensor(x[:], x[:], bcast[:, 2, :].unsqueeze(1).to_broadcast([P, TILES, P]),
                               ALU.add).then_inc(xb_ready, 1)

        @block.scalar
        def _(act):
            act.sem_inc(ring_taken, SLOTS)

            def weights():
                act.wait_ge(w_loaded, 9 * 16)
                for i in range(2):
                    pair = wa[:, i, :].rearrange("p (n two) -> p n two", two=2)
                    swap = wsw[:, i, :].rearrange("p (n two) -> p n two", two=2)
                    act.copy(swap[:, :, 0], pair[:, :, 1])
                    act.copy(swap[:, :, 1], pair[:, :, 0])
                act.wait_ge(weights_turned, 1)
                act.copy(wfT[:].rearrange("p k n -> p (k n)"), out_bank(1)[:, 0:3 * P]).then_inc(weights_done, 1)

            def layer_norm(layer):
                act.wait_ge(var_ready, layer + 1)
                act.activation(std[:], veps[:], ACT.Sqrt).then_inc(std_ready, 1)
                for c in range(CHUNKS):
                    copy_turned(CHUNKS * (layer + (layer + 1) // 2) + c, c)

            def copy_turned(n, c):
                act.wait_ge(turned, n + 1)
                act.copy(xnT[:, 1 + c * CHUNK:1 + (c + 1) * CHUNK], turn_bank(c)).then_inc(turned_copied, 1)

            def split():
                for n in range(2 * CHUNKS + 1):
                    if n < 2 * CHUNKS:
                        c, kq = n // 2, n % 2
                        act.wait_ge(comb_ready, n + 1)
                        act.copy(parts[kq][:, 0, c * CHUNK:(c + 1) * CHUNK], comb[:, n % 2, :]).then_inc(hi_ready, 1)
                    if n >= 1:
                        c, kq = (n - 1) // 2, (n - 1) % 2
                        act.wait_ge(resid_ready, n)
                        act.copy(parts[kq][:, 1, c * CHUNK:(c + 1) * CHUNK],
                                 resid[:, (n - 1) % 2, :]).then_inc(mid_ready, 1)

            def copy_max(unit, half):
                act.wait_ge(ring_ready, max_item(unit, half) + 1)
                act.copy(qst[MROW:MROW + 3, bass.ds((unit // CHUNKS) % 2, 1), 2 * half:2 * half + 2,
                             bass.ds(unit % CHUNKS, 1), :],
                         max_rows(max_slot(unit, half)).rearrange("p (a j c t) -> p a j c t", a=1, j=2, c=1)
                         ).then_inc(ring_taken, 1)

            def copy_acc(unit):
                act.wait_ge(pv_done, unit * STEPS + (STEPS + RING))
                act.copy(o_unit[:], acc).then_inc(o_copied, 1)

            def copy_turned_output(unit, last):
                act.wait_ge(o_turned, unit + 1)
                act.wait_ge(o_done, unit + 1)
                act.copy(o_tok[:], psum[:, turned_slot(last), :].rearrange(
                    "p (s e) -> p s e", e=STRIP)[:, :, 0:VW]).then_inc(o_taken, 1)

            def unit_body(unit, has_next, has_second, has_before):
                for t in range(STEPS):
                    for j in range(HG):
                        if t == TURN_STEP and j == HG - 1 and has_before:
                            copy_turned_output(unit - 1, False)
                        act.wait_ge(ring_ready, item(unit, t, j) + 1)
                        if j == 0:
                            act.wait_ge(pv_done, unit * STEPS + (t + 1))
                        act.activation(probs[:, t % RING, j * CHUNK:(j + 1) * CHUNK], psum[:, slot(unit, t, j), :],
                                       ACT.Exp, scale=SCALE).then_inc(ring_taken, 1)
                    if t == LAG - 1 and has_before:
                        copy_acc(unit - 1)
                    if has_next and t in MAX_STEPS:
                        copy_max(unit + 1, MAX_STEPS.index(t))

            def finish_attention(c0):
                for c in range(CHUNKS):
                    copy_turned(c0 + c, c)

            def ffn(f):
                for c in range(CHUNKS):
                    n = CHUNKS * f + c
                    act.wait_ge(rk_ready, n + 1)
                    if c >= 2:
                        act.wait_ge(x_new, CHUNKS * (2 * f + 1) + c - 1)
                        act.wait_ge(kv_ready, n - 1)
                    act.activation(gate[:, c % 2, :], proj_bank(c), ACT.Sigmoid).then_inc(gate_ready, 1)
                    act.activation(relu[:, c % 2, :], swap_bank(c), ACT.Relu).then_inc(relu_ready, 1)
                    act.wait_ge(relu_ready, n + 1)
                    act.activation(act2[:, c % 2, :], relu[:, c % 2, :], ACT.Square).then_inc(act_ready, 1)

            def head_attention():
                for c in range(CHUNKS + 1):
                    for i in range(TPC if c < CHUNKS else 0):
                        n = TPC * c + i
                        act.wait_ge(qkv_ready, n + 1)
                        act.copy(qkv[:, n, :], qkv_bank(n)).then_inc(qkv_copied, 1)
                for c in range(CHUNKS):
                    act.wait_ge(hs_ready, c + 1)
                    act.activation(he[:, c * TPC:(c + 1) * TPC, :], hs[:, c * TPC:(c + 1) * TPC, :],
                                   ACT.Exp, scale=SCALE).then_inc(he_ready, 1)

            layer_norm(0)
            weights()
            split()
            copy_max(0, 0)
            copy_max(0, 1)
            attention_units(act, unit_body)
            copy_acc(UNITS - 1)
            copy_turned_output(UNITS - 1, True)
            finish_attention(CHUNKS)
            layer_norm(1)
            ffn(0)
            layer_norm(2)
            head_attention()
            finish_attention(4 * CHUNKS)
            layer_norm(3)
            ffn(1)

        @block.vector
        def _(dve):
            steps = [0]

            def step(ins):
                steps[0] += 1
                ins.then_inc(dve_step, 1)
                return steps[0]

            dve.sem_inc(sm_free, 2)
            dve.sem_inc(o_done, 1)
            dve.memset(xnT[:, 0:1], 0.0)
            step(dve.memset(v_all[:].rearrange("p (n e) -> p n e", e=VW)[:, :, HD:VW], 1.0))

            def vectors():
                dve.wait_ge(rows_loaded, 8 * 16)
                pair = rows[0:1, BQ:BK + 1, :].rearrange("p k (n two) -> p k n two", two=2)
                swap = rows[0:1, BQ_SWAP:BK_SWAP + 1, :].rearrange("p k (n two) -> p k n two", two=2)
                dve.tensor_copy(swap[:, :, :, 0], pair[:, :, :, 1])
                dve.tensor_copy(swap[:, :, :, 1], pair[:, :, :, 0]).then_inc(rows_done, 1)
                dve.wait_ge(vectors_spread, 1)
                dve.tensor_copy(bcast[:].rearrange("p k n -> p (k n)"), swap_bank(1)[:, 0:3 * P])
                done = step(dve.tensor_copy(cols[:], out_bank(0)[:, 0:N_COLS]))
                dve.wait_ge(dve_step, done)
                dve.tensor_scalar(omu[:], cols[:, MU_R:MU_K + 1], -1.0, 1.0, ALU.mult, ALU.add).then_inc(vectors_done, 1)

            def layer_norm(layer):
                for n in range(TILES):
                    if n % TPC == 0:
                        if layer == 0:
                            dve.wait_ge(x_loaded, 16 * CHUNKS)
                        else:
                            dve.wait_ge(x_new, CHUNKS * (layer - 1) + n // TPC + 1)
                    done = step(dve.bn_stats(stats[:, n, :], x[:, n, :]))
                dve.wait_ge(dve_step, done)
                for n in range(TILES):
                    done = step(dve.bn_aggr(mv[:, n, :], stats[:, n, :]))
                dve.wait_ge(dve_step, done)
                dve.tensor_scalar(veps[:], mv[:, :, 1], EPS, None, ALU.add).then_inc(var_ready, 1)
                dve.wait_ge(std_ready, layer + 1)
                done = step(dve.reciprocal(rstd[:], std[:]))
                dve.wait_ge(dve_step, done)
                for n in range(TILES):
                    last = dve.tensor_scalar(xn[:, n, :], x[:, n, :], mv[:, n, 0:1], rstd[:, n:n + 1],
                                             ALU.subtract, ALU.mult)
                    if n % TPC == TPC - 1:
                        last.then_inc(xn_ready, 1)

            def projections():
                col = (BK, BQ)

                def combine(n):
                    c, kq = n // 2, n % 2
                    cs = slice(c * CHUNK, (c + 1) * CHUNK)
                    dve.wait_ge(proj_ready, n + 1)
                    bias = cols[:, col[kq]:col[kq] + 1]
                    if n >= 1:
                        dve.wait_ge(comb_ready, n)
                    dve.scalar_tensor_tensor(out=rope1, in0=proj_bank(n), scalar=bias, in1=cos[:, cs],
                                             op0=ALU.add, op1=ALU.mult)
                    done = step(dve.scalar_tensor_tensor(
                        out=rope2, in0=swap_bank(n), scalar=cols[:, col[kq] + 2:col[kq] + 3],
                        in1=sin[:, cs], op0=ALU.add, op1=ALU.mult))
                    dve.wait_ge(dve_step, done)
                    if n >= 2:
                        dve.wait_ge(resid_ready, n - 1)
                        dve.wait_ge(hi_ready, n - 1)
                    dve.tensor_tensor(comb[:, n % 2, :], rope1, rope2, ALU.add).then_inc(comb_ready, 1)

                def residual(n):
                    c, kq = n // 2, n % 2
                    dve.wait_ge(hi_ready, n + 1)
                    if n >= 2:
                        dve.wait_ge(lo_ready, n - 1)
                        dve.wait_ge(mid_ready, n - 1)
                    dve.tensor_tensor(resid[:, n % 2, :], comb[:, n % 2, :],
                                      parts[kq][:, 0, c * CHUNK:(c + 1) * CHUNK], ALU.subtract).then_inc(resid_ready, 1)

                def low(n):
                    c, kq = n // 2, n % 2
                    dve.wait_ge(mid_ready, n + 1)
                    dve.tensor_tensor(parts[kq][:, 2, c * CHUNK:(c + 1) * CHUNK], resid[:, n % 2, :],
                                      parts[kq][:, 1, c * CHUNK:(c + 1) * CHUNK], ALU.subtract).then_inc(lo_ready, 1)

                dve.wait_ge(trig_loaded, 32)
                for n in range(2 * CHUNKS + 2):
                    if n < 2 * CHUNKS:
                        combine(n)
                    if 1 <= n <= 2 * CHUNKS:
                        residual(n - 1)
                    if n >= 2:
                        low(n - 2)
                    if n % 2 == 1 and n < 2 * CHUNKS:
                        c = n // 2
                        dve.wait_ge(v_ready, c + 1)
                        v_dst = v_all[:].rearrange("p (g t j e) -> p t g j e", g=GROUPS, t=TILES, j=HG)
                        for i in range(TPC):
                            last = dve.tensor_tensor(
                                v_dst[:, TPC * c + i, :, :, 0:HD],
                                out_bank(c)[:, i * P:(i + 1) * P].rearrange("p (g j d) -> p g j d", g=GROUPS, j=HG),
                                bcast[:, 0, :].rearrange("p (g j d) -> p g j d", g=GROUPS, j=HG), ALU.add)
                        last.then_inc(v_used, 1)

            def take_max(unit, r, kc):
                dve.wait_ge(sm_ready, unit * ROWS * KC + (KC * r + kc + 1))
                if r == 0 and kc == 0 and not (isinstance(unit, int) and unit == 0):
                    dve.wait_ge(max_step, unit * MSTEPS - (MSTEPS - 1))
                dve.tensor_reduce(mpart[:, KC * r + kc:KC * r + kc + 1], sm_banks(kc), AX_X,
                                  ALU.max).then_inc(sm_free, 1)

            def max_parts(unit, i):
                def wait_step(k):
                    dve.wait_ge(max_step, unit * MSTEPS + k)

                if i == 0:
                    dve.wait_ge(sm_free, unit * ROWS * KC + (ROWS * KC + 2))
                    dve.tensor_reduce(nmax[:], mpart[:].rearrange("p (r k) -> p r k", k=KC), AX_X, ALU.max,
                                      negate=True).then_inc(max_step, 1)
                if i == 1:
                    wait_step(1)
                    dve.tensor_copy(nmax_p[:, :, 0], nmax[:]).then_inc(max_step, 1)
                if i == 2:
                    wait_step(2)
                    dve.tensor_tensor(nmax_r[:, 0, :], nmax[:], nmax_p[:, :, 0], ALU.subtract).then_inc(max_step, 1)
                if i == 3:
                    wait_step(3)
                    dve.tensor_copy(nmax_p[:, :, 1], nmax_r[:, 0, :]).then_inc(max_step, 1)
                if i == 4:
                    wait_step(4)
                    dve.tensor_tensor(nmax_r[:, 1, :], nmax_r[:, 0, :], nmax_p[:, :, 1],
                                      ALU.subtract).then_inc(max_step, 1)
                if i == 5:
                    wait_step(5)
                    dve.tensor_copy(nmax_p[:, :, 2], nmax_r[:, 1, :]).then_inc(max_step, 1)

            def norm_recip(unit):
                dve.wait_ge(o_taken, unit + 1)
                dve.reciprocal(rden[:].unsqueeze(2), o_tok[:, :, HD:VW]).then_inc(rden_ready, 1)

            def norm_mul(unit):
                dve.wait_ge(rden_ready, unit + 1)
                dve.tensor_tensor(
                    attn[:, bass.ds((unit % CHUNKS) * TPC, TPC), bass.ds((unit // CHUNKS) * (HG * HD), HG * HD)
                         ].rearrange("p q (j d) -> p q j d", j=HG),
                    o_tok[:, :, 0:HD].rearrange("p (q j) d -> p q j d", q=TPC),
                    rden[:].rearrange("p (q j e) -> p q j e", q=TPC, e=1).to_broadcast([P, TPC, HG, HD]),
                    ALU.mult).then_inc(o_done, 1)

            def unit_body(unit, has_next, has_second, has_before):
                for t in range(STEPS):
                    there = has_next if t < STEPS - LEAD else has_second
                    for kc in range(KC):
                        if there:
                            v, r = max_row(unit, t)
                            take_max(v, r, kc)
                        if has_before and t == TURN_STEP + 1 and kc == 0:
                            norm_recip(unit - 1)
                        if has_before and t == TURN_STEP + 1 and kc == 1:
                            norm_mul(unit - 1)
                        k = (t - (STEPS - LEAD)) * KC + kc + 1
                        if has_next and 0 <= k < MSTEPS // 2:
                            max_parts(unit + 1, 2 * k)
                            max_parts(unit + 1, 2 * k + 1)

            def attention():
                for r in range(ROWS):
                    for kc in range(KC):
                        take_max(0, r, kc)
                for i in range(MSTEPS):
                    max_parts(0, i)
                for r in range(LEAD):
                    for kc in range(KC):
                        take_max(1, r, kc)
                attention_units(dve, unit_body)
                norm_recip(UNITS - 1)
                norm_mul(UNITS - 1)

            def head_attention():
                head = qkv.rearrange("p n (h e) -> p n h e", h=H)
                done = {}

                def wait_summed(i):
                    if summed_by_dve(*items[i]):
                        dve.wait_ge(dve_summed, i + 1 - (len(items) - TPC))
                    else:
                        dve.wait_ge(pe_summed, i + 1)

                def products(i, kind, n):
                    buf = i % 3
                    if i >= 3:
                        wait_summed(i - 3)
                    if kind == "qk":
                        dve.wait_ge(qkv_copied, n + 1)
                        shape = [P, HD, H, H]
                        in0 = head[:, n, :, 0:HD].rearrange("p h d -> p d h").unsqueeze(3).to_broadcast(shape)
                        in1 = head[:, n, :, HD:2 * HD].rearrange("p g d -> p d g").unsqueeze(2).to_broadcast(shape)
                        dst = prod[:, buf, :].rearrange("p (d h g) -> p d h g", h=H, g=H)
                    else:
                        if n % TPC == 0:
                            dve.wait_ge(he_ready, n // TPC + 1)
                        shape = [P, H, H, HD]
                        in0 = he[:, n, :].rearrange("p (h g) -> p g h", h=H).unsqueeze(3).to_broadcast(shape)
                        in1 = head[:, n, :, 2 * HD:3 * HD].unsqueeze(2).to_broadcast(shape)
                        dst = prod[:, buf, :].rearrange("p (g h d) -> p g h d", g=H, h=H)
                    dve.tensor_tensor(dst, in0, in1, ALU.mult).then_inc(prod_ready, 1)

                def sums(i, kind, n):
                    dve.wait_ge(prod_ready, i + 1)
                    dve.tensor_reduce(ctx_raw[:, n % TPC, :], prod[:, i % 3, :].rearrange("p (g s) -> p s g", g=H),
                                      AX_X, ALU.add).then_inc(dve_summed, 1)

                def shift(i, c):
                    wait_summed(i)
                    sc = hs_banks(c).rearrange("p (s g) -> p s g", g=H)
                    got = step(dve.tensor_reduce(hmax[:], sc, AX_X, ALU.max))
                    dve.wait_ge(dve_step, got)
                    dve.tensor_tensor(hs[:, c * TPC:(c + 1) * TPC, :].rearrange("p n (h g) -> p (n h) g", h=H), sc,
                                      hmax[:].unsqueeze(2).to_broadcast([P, TPC * H, H]),
                                      ALU.subtract).then_inc(hs_ready, 1)

                def denominators(c):
                    dve.wait_ge(he_ready, c + 1)
                    if c >= 1:
                        dve.wait_ge(ctx_ready, c)
                    got = step(dve.tensor_reduce(hden[:], he[:, c * TPC:(c + 1) * TPC, :].rearrange(
                        "p n (h g) -> p (n h) g", h=H), AX_X, ALU.add))
                    dve.wait_ge(dve_step, got)
                    done[c] = step(dve.reciprocal(hrden[:], hden[:]))

                def divide(i, c):
                    wait_summed(i)
                    dve.wait_ge(dve_step, done[c])
                    raw = ctx_raw.rearrange("p n d -> p (n d)") if summed_by_dve("pv", TPC * c) else out_bank(c)
                    dve.tensor_tensor(attn[:, c * TPC:(c + 1) * TPC, :].rearrange("p n (h d) -> p (n h) d", h=H),
                                      raw.rearrange("p (s d) -> p s d", d=HD),
                                      hrden[:].unsqueeze(2).to_broadcast([P, TPC * H, HD]),
                                      ALU.mult).then_inc(ctx_ready, 1)

                for i in range(len(items) + 2):
                    if i < len(items):
                        products(i, *items[i])
                        if i >= 1 and summed_by_dve(*items[i - 1]):
                            sums(i - 1, *items[i - 1])
                    if i == len(items):
                        sums(i - 1, *items[i - 1])
                    kind, n = items[i - 2] if i >= 2 else (None, 0)
                    if n % TPC == TPC - 1:
                        if kind == "qk":
                            shift(i - 2, n // TPC)
                        else:
                            divide(i - 2, n // TPC)
                    if i < len(items) and items[i][0] == "pv" and items[i][1] % TPC == TPC - 1:
                        denominators(items[i][1] // TPC)

            def output_projection(a):
                dve.wait_ge(xb_ready, a + 1)
                for c in range(CHUNKS):
                    dve.wait_ge(op_ready, CHUNKS * a + c + 1)
                    xc = x[:, c * TPC:(c + 1) * TPC, :].rearrange("p n d -> p (n d)")
                    dve.tensor_tensor(xc, out_bank(c), xc, ALU.add).then_inc(x_new, 1)

            def ffn(a):
                layer = 2 * a + 1

                def mixes(c):
                    dve.wait_ge(turned_copied, CHUNKS * (3 * a + 2) + c + 1)
                    if c >= 2:
                        dve.wait_ge(rk_ready, CHUNKS * a + c - 1)
                    cur = xnT[:, 1 + c * CHUNK:1 + (c + 1) * CHUNK]
                    prev = xnT[:, c * CHUNK:(c + 1) * CHUNK]
                    dve.tensor_scalar(ffn_r[:, c % 2, :], cur, cols[:, MU_R:MU_R + 1], None, ALU.mult)
                    done = step(dve.tensor_scalar(ffn_k[:, c % 2, :], cur, cols[:, MU_K:MU_K + 1], None, ALU.mult))
                    dve.wait_ge(dve_step, done)
                    dve.scalar_tensor_tensor(out=ffn_r[:, c % 2, :], in0=prev, scalar=omu[:, 0:1],
                                             in1=ffn_r[:, c % 2, :], op0=ALU.mult, op1=ALU.add)
                    dve.scalar_tensor_tensor(out=ffn_k[:, c % 2, :], in0=prev, scalar=omu[:, 1:2],
                                             in1=ffn_k[:, c % 2, :], op0=ALU.mult, op1=ALU.add).then_inc(mixed, 1)

                def gated(c):
                    dve.wait_ge(kv_ready, CHUNKS * a + c + 1)
                    dve.wait_ge(gate_ready, CHUNKS * a + c + 1)
                    done = step(dve.tensor_tensor(gate[:, c % 2, :], out_bank(c), gate[:, c % 2, :], ALU.mult))
                    dve.wait_ge(dve_step, done)
                    xc = x[:, c * TPC:(c + 1) * TPC, :].rearrange("p n d -> p (n d)")
                    dve.tensor_tensor(xc, gate[:, c % 2, :], xc, ALU.add).then_inc(x_new, 1)

                for c in range(CHUNKS + 1):
                    if c < CHUNKS:
                        mixes(c)
                    if c >= 1:
                        gated(c - 1)

            layer_norm(0)
            vectors()
            projections()
            attention()
            output_projection(0)
            layer_norm(1)
            ffn(0)
            layer_norm(2)
            head_attention()
            output_projection(1)
            layer_norm(3)
            ffn(1)

        @block.tensor
        def _(pe):
            pe.sem_inc(pv_done, RING)
            pe.wait_ge(ident_ready, 1)

            def setup():
                pe.wait_ge(w_loaded, 9 * 16)
                for i in range(3):
                    last = pe.transpose(out_bank(1)[:, i * P:(i + 1) * P], wf_in[:, i, :], ident[:])
                last.then_inc(weights_turned, 1)
                pe.wait_ge(rows_done, 1)
                for i in range(N_COLS):
                    pe.matmul(out_bank(0)[:, i:i + 1], rows[0:1, i, :], ones_row[0:1, 0:1], start=True, stop=True)
                for i in range(3):
                    last = pe.matmul(swap_bank(1)[:, i * P:(i + 1) * P], ones_row[:], rows[0:1, N_COLS + i, :],
                                     start=True, stop=True)
                last.then_inc(vectors_spread, 1)

            def turn(tile_of, n, c):
                if c >= 2:
                    pe.wait_ge(turned_copied, n - 1)
                for i in range(TPC):
                    last = pe.transpose(turn_bank(c)[:, i * P:(i + 1) * P], tile_of(TPC * c + i), ident[:])
                last.then_inc(turned, 1)

            def layer_norm(layer):
                for c in range(CHUNKS):
                    pe.wait_ge(xn_ready, CHUNKS * layer + c + 1)
                    turn(lambda i: xn[:, i, :], CHUNKS * (layer + (layer + 1) // 2) + c, c)

            def projections():
                w = (wa[:, 1, :], wa[:, 0, :])
                w_v = wa[:, 2, :]
                pe.wait_ge(weights_done, 1)
                pe.wait_ge(vectors_done, 1)
                for c in range(CHUNKS):
                    pe.wait_ge(turned_copied, c + 1)
                    xc = xnT[:, 1 + c * CHUNK:1 + (c + 1) * CHUNK]
                    for kq in range(2):
                        n = 2 * c + kq
                        if n >= 2:
                            pe.wait_ge(comb_ready, n - 1)
                        pe.matmul(proj_bank(n), w[kq], xc, start=True, stop=True)
                        pe.matmul(swap_bank(n), wsw[:, 1 - kq, :], xc, start=True,
                                  stop=True).then_inc(proj_ready, 1)
                    if c >= 2:
                        pe.wait_ge(v_used, c - 1)
                    for i in range(TPC):
                        last = pe.matmul(out_bank(c)[:, i * P:(i + 1) * P], xc[:, i * P:(i + 1) * P], w_v,
                                         start=True, stop=True)
                    last.then_inc(v_ready, 1)

            def max_scores(unit, r, kc):
                j, qt = r // TPC, r % TPC
                pe.wait_ge(sm_free, unit * ROWS * KC + (KC * r + kc + 1))
                for i in range(KW // CHUNK):
                    last = pe.matmul(sm_banks(kc)[:, i * CHUNK:(i + 1) * CHUNK], q_cols(unit, j, qt * P, P),
                                     k_cols(unit, j, kc * KW + i * CHUNK, CHUNK), start=True, stop=True)
                last.then_inc(sm_ready, 1)

            def scores(unit, t, j):
                pe.wait_ge(ring_taken, item(unit, t, j) + 1)
                pe.matmul(psum[:, slot(unit, t, j), :], k_cols(unit, j, t * P, P), q_cols(unit, j, 0, CHUNK),
                          start=True, stop=True).then_inc(ring_ready, 1)

            def product_v(unit, t):
                if t == 0:
                    pe.wait_ge(v_unit_ready, unit * 2 + 1)
                if t == STEPS - LAG:
                    pe.wait_ge(v_unit_ready, unit * 2 + 2)
                pe.wait_ge(ring_taken, item(unit, t, HG - 1) + (1 + SLOTS))
                for j in range(HG):
                    last = pe.matmul(acc[STRIP * j:STRIP * (j + 1), :], v_unit[:, t, j, :],
                                     probs[:, t % RING, j * CHUNK:(j + 1) * CHUNK],
                                     start=(t == 0), stop=(t == STEPS - 1))
                last.then_inc(pv_done, 1)

            def turn_output(unit, last_unit):
                pe.wait_ge(o_copied, unit + 1)
                pe.wait_ge(ring_taken, TOTAL_ITEMS - 1 + SLOTS if last_unit
                           else item(unit + 1, TURN_STEP, HG - 1) + (SLOTS - 1))
                for q in range(TPC):
                    last = pe.transpose(psum[:, turned_slot(last_unit), q * P:(q + 1) * P],
                                        o_unit[:, q * P:(q + 1) * P], ident[:])
                last.then_inc(o_turned, 1)

            def turn_max(unit, half):
                if half == 0:
                    pe.wait_ge(max_step, unit * MSTEPS + MSTEPS)
                pe.wait_ge(ring_taken, max_item(unit, half) + 1)
                for i in range(ROWS // 2):
                    last = pe.transpose(max_rows(max_slot(unit, half))[:, i * P:(i + 1) * P],
                                        nmax_p[:, half * (ROWS // 2) + i, :], ident_b[:])
                last.then_inc(ring_ready, 1)

            def unit_body(unit, has_next, has_second, has_before):
                for t in range(STEPS):
                    there = has_next if t < STEPS - LEAD else has_second
                    v, r = max_row(unit, t)
                    if t == STEPS - LEAD and has_second:
                        pe.wait_ge(stacks_ready, (unit + 2) // CHUNKS + 1)
                    if there:
                        max_scores(v, r, 0)
                    if t == TURN_STEP + 1 and has_before:
                        pe.wait_ge(o_taken, unit)
                    scores(unit, t, 0)
                    scores(unit, t, 1)
                    scores(unit, t, 2)
                    if there:
                        max_scores(v, r, 1)
                    if t >= LAG:
                        if t == LAG and has_before:
                            pe.wait_ge(o_copied, unit)
                        product_v(unit, t - LAG)
                    elif has_before:
                        product_v(unit - 1, t + (STEPS - LAG))
                    if t == TURN_STEP and has_before:
                        turn_output(unit - 1, False)
                    scores(unit, t, 3)
                    if has_next and t in MAX_STEPS:
                        turn_max(unit + 1, MAX_STEPS.index(t))

            def attention():
                pe.wait_ge(stacks_ready, 1)
                for r in range(ROWS):
                    for kc in range(KC):
                        max_scores(0, r, kc)
                for r in range(LEAD):
                    for kc in range(KC):
                        max_scores(1, r, kc)
                    if r == 1:
                        turn_max(0, 0)
                turn_max(0, 1)
                pe.wait_ge(ring_taken, SLOTS + 2)
                attention_units(pe, unit_body)
                for t in range(STEPS - LAG, STEPS):
                    product_v(UNITS - 1, t)
                turn_output(UNITS - 1, True)

            def head_qkv():
                for n in range(TILES):
                    pe.wait_ge(turned_copied, 3 * CHUNKS + n // TPC + 1)
                    if n >= 4:
                        pe.wait_ge(qkv_copied, n - 3)
                    first = 1 + n * P
                    pe.matmul(qkv_bank(n), xnT[:, first:first + P], wqkv[:], start=True, stop=False)
                    pe.matmul(qkv_bank(n), ones_row[:], rows[0:1, B_QKV:N_ROWS, :].rearrange("p k d -> p (k d)"),
                              start=False, stop=True).then_inc(qkv_ready, 1)

            def head_sums():
                for i, (kind, n) in enumerate(items):
                    if summed_by_dve(kind, n):
                        continue
                    c = n // TPC
                    if kind == "qk":
                        if n % TPC == 0 and c >= 2:
                            pe.wait_ge(hs_ready, c - 1)
                        dst, terms = hs_banks(c)[:, (n % TPC) * H * H:(n % TPC + 1) * H * H], HD
                    else:
                        if n % TPC == 0 and c >= 2:
                            pe.wait_ge(ctx_ready, c - 1)
                        dst, terms = out_bank(c)[:, (n % TPC) * P:(n % TPC + 1) * P], H
                    pe.wait_ge(prod_ready, i + 1)
                    w = H * H * HD // terms
                    for k in range(terms):
                        last = pe.matmul(dst, ident[:], prod[:, i % 3, k * w:(k + 1) * w],
                                         start=(k == 0), stop=(k == terms - 1))
                    last.then_inc(pe_summed, 1)

            def output_projection(a):
                if a == 0:
                    pe.wait_ge(o_done, UNITS + 1)
                for c in range(CHUNKS):
                    if a == 1:
                        pe.wait_ge(ctx_ready, c + 1)
                    turn(lambda i: attn[:, i, :], CHUNKS * (3 * a + 1) + c, c)
                for c in range(CHUNKS):
                    pe.wait_ge(turned_copied, CHUNKS * (3 * a + 1) + c + 1)
                    if c >= 2:
                        pe.wait_ge(x_new, CHUNKS * 2 * a + c - 1)
                    for i in range(TPC):
                        first = 1 + (TPC * c + i) * P
                        last = pe.matmul(out_bank(c)[:, i * P:(i + 1) * P], xnT[:, first:first + P],
                                         (wa[:, 3, :], wout[:])[a], start=True, stop=True)
                    last.then_inc(op_ready, 1)

            def ffn(a):
                def gates(c):
                    pe.wait_ge(mixed, CHUNKS * a + c + 1)
                    if c >= 2:
                        pe.wait_ge(relu_ready, CHUNKS * a + c - 1)
                    for i in range(TPC):
                        pe.matmul(proj_bank(c)[:, i * P:(i + 1) * P], ffn_r[:, c % 2, i * P:(i + 1) * P],
                                  wfT[:, 0, :], start=True, stop=True)
                    pe.matmul(swap_bank(c), wfT[:, 1, :], ffn_k[:, c % 2, :], start=True,
                              stop=True).then_inc(rk_ready, 1)

                def values(c):
                    pe.wait_ge(act_ready, CHUNKS * a + c + 1)
                    if c >= 2:
                        pe.wait_ge(x_new, CHUNKS * (2 * a + 1) + c - 1)
                    for i in range(TPC):
                        last = pe.matmul(out_bank(c)[:, i * P:(i + 1) * P], act2[:, c % 2, i * P:(i + 1) * P],
                                         wfT[:, 2, :], start=True, stop=True)
                    last.then_inc(kv_ready, 1)

                for c in range(CHUNKS + 1):
                    if c < CHUNKS:
                        gates(c)
                    if c >= 1:
                        values(c - 1)

            layer_norm(0)
            setup()
            projections()
            attention()
            output_projection(0)
            layer_norm(1)
            ffn(0)
            layer_norm(2)
            head_qkv()
            pe.wait_ge(qkv_copied, TILES)
            head_sums()
            output_projection(1)
            layer_norm(3)
            ffn(1)


def rope_tables():
    inv_freq = (np.float32(1.0) / np.float32(ROPE_BASE) ** (np.arange(0, HD, 2, dtype=np.float32) / np.float32(HD)))
    freqs = np.arange(S, dtype=np.float32)[:, None] * inv_freq.astype(np.float32)
    cos = np.repeat(np.cos(freqs), 2, axis=-1).T
    sin = np.repeat(np.sin(freqs), 2, axis=-1).T
    sign = np.where(np.arange(HD) % 2 == 0, np.float32(-1.0), np.float32(1.0))[:, None]
    return (np.ascontiguousarray(np.tile(cos, (H, 1)).astype(np.float32)),
            np.ascontiguousarray(np.tile(sin * sign, (H, 1)).astype(np.float32)))


COS, SIN = rope_tables()
ZERO_ROWS = np.zeros((3, HG * S // 2), np.float32)

_INS = ['L0_attn_a_x', 'L0_attn_a_Wq', 'L0_attn_a_bq', 'L0_attn_a_Wk', 'L0_attn_a_bk', 'L0_attn_a_Wv',
        'L0_attn_a_bv', 'L0_attn_a_Wp', 'L0_attn_a_bp', 'L0_attn_b_W_qkv', 'L0_attn_b_b_qkv',
        'L0_attn_b_W_out', 'L0_attn_b_b_out', 'L0_ffn_W_r', 'L0_ffn_W_k', 'L0_ffn_W_v', 'L0_ffn_mu_r',
        'L0_ffn_mu_k']


def kernel(**inputs):
    import concourse.bacc as _bacc
    from concourse.bass_utils import run_bass_kernel_spmd as _run

    nc = _bacc.Bacc("TRN2", target_bir_lowering=False, num_devices=1)
    arrays, args = {}, []
    named = {n: np.ascontiguousarray(inputs[n]) for n in _INS}
    named['L0_attn_a_x'] = named['L0_attn_a_x'].reshape(S, P)
    named.update(rope_cos=COS, rope_sin=SIN, zero_rows=ZERO_ROWS)
    for name, a in named.items():
        arrays[f"in_{name}"] = a
        args.append(nc.dram_tensor(f"in_{name}", a.shape, mybir.dt.from_np(a.dtype), kind="ExternalInput").ap())
    args.append(nc.dram_tensor("out_x", (S, P), F32, kind="ExternalOutput").ap())
    build(nc, *args)
    r = _run(nc, [arrays], core_ids=[0])
    return r.results[0]["out_x"].reshape(1, S, P)
```

```python
from contextlib import ExitStack

import numpy as np

import concourse.bass as bass
from concourse import mybir

F32 = mybir.dt.float32
BF16 = mybir.dt.bfloat16
ALU = mybir.AluOpType
ACT = mybir.ActivationFunctionType
AX_X = mybir.AxisListType.X

P = 128
S = 2048
H, HD = 16, 8
TILES = S // P
CHUNK = 512
CHUNKS = S // CHUNK
TPC = CHUNK // P
HG = 4
GROUPS = H // HG
UNITS = GROUPS * CHUNKS
STEPS = TILES
ROWS = HG * TPC
KC = 2
KW = S // KC
LEAD = 4
FIRST_LEAD = 2
LAG = 2
SLOTS = 3
MAX_STEPS = (STEPS - 3, STEPS - 2)
ITEMS = HG * STEPS + 2
TOTAL_ITEMS = UNITS * ITEMS
TURN_STEP = 3
RING = 4
VW = HD + 1
STRIP = 32
RUNS = ((0, 3, 0), (3, 2, 1), (5, 1, 2))
MROW = 64
SCALE = float(1.0 / np.sqrt(HD))
EPS = 1e-5
ROPE_BASE = 10000.0

(BQ, BK, BQ_SWAP, BK_SWAP, MU_R, MU_K, BV, BP, B_OUT, B_QKV) = range(10)
N_COLS = 6
N_ROWS = 12


def build(nc, x_in, wq, bq, wk, bk, wv, bv, wp, bp, w_qkv, b_qkv, w_out, b_out,
          w_r, w_k, w_v, mu_r, mu_k, cos_t, sin_t, zero_rows, out):
    with ExitStack() as ctx:
        def sb(name, shape, dt):
            return ctx.enter_context(nc.sbuf_tensor(name, shape, dt))

        def sem(name):
            return ctx.enter_context(nc.semaphore(name))

        psum = ctx.enter_context(nc.psum_tensor("psum", [P, 8, CHUNK], F32))

        x = sb("x", [P, TILES, P], F32)
        xnT = sb("xnT", [P, 1 + S], F32)
        attn = sb("attn", [P, TILES, P], F32)
        xn = attn
        kst = sb("kst", [P, 2 * HG * S], BF16)
        qst = sb("qst", [P, 2, HG, CHUNKS, CHUNK], BF16)
        qflat = qst[:].rearrange("p a j c t -> p (a j c t)")
        probs = sb("probs", [P, RING, HG * CHUNK], F32)
        v_all = sb("v_all", [P, GROUPS * TILES * HG * VW], F32)
        v_unit = sb("v_unit", [P, TILES, HG, STRIP], F32)
        o_unit = sb("o_unit", [P, CHUNK], F32)
        parts = [sb("k_parts", [P, 3, S], BF16), sb("q_parts", [P, 3, S], BF16)]

        def in_probs(slot, half):
            return probs[:, slot, half * 2 * CHUNK:(half + 1) * 2 * CHUNK].rearrange("p (b t) -> p b t", b=2)

        cos = probs[:, 0, :]
        sin = probs[:, 1, :]
        comb = in_probs(2, 0)
        rope1 = in_probs(2, 1)[:, 0, :]
        rope2 = in_probs(2, 1)[:, 1, :]
        resid = in_probs(3, 0)
        ffn_k = in_probs(0, 1)
        gate = in_probs(1, 0)
        relu = in_probs(1, 1)
        act2 = in_probs(2, 0)
        qkv = kst[:].bitcast(F32)[:, 0:TILES * 3 * P].rearrange("p (n e) -> p n e", n=TILES)
        prod = probs
        he = qflat.bitcast(F32)[:, 0:TILES * H * H].rearrange("p (n e) -> p n e", n=TILES)
        ctx_raw = parts[0][:].rearrange("p s t -> p (s t)").bitcast(F32)[:, 0:TPC * P].rearrange(
            "p (n e) -> p n e", n=TPC)
        hs_raw = parts[1][:].rearrange("p s t -> p (s t)").bitcast(F32)[:, 0:2 * 2 * H * H].rearrange(
            "p (b n e) -> p b n e", b=2, n=2)
        hmax = sb("hmax", [P, CHUNKS, TPC * H], F32)
        hbias = sb("hbias", [P, CHUNKS, TPC * H], F32)
        hden = sb("hden", [P, CHUNKS, TPC * H], F32)
        hrden = sb("hrden", [P, TPC * H], F32)
        wa = sb("wa", [P, 4, P], F32)
        wsw = sb("wsw", [P, 2, P], F32)
        wqkv = sb("wqkv", [P, 3 * P], F32)
        wout = sb("wout", [P, P], F32)
        wf_in = sb("wf_in", [P, 3, P], F32)
        wfT = sb("wfT", [P, 3, P], F32)
        wr_mu = sb("wr_mu", [P, 2, P], F32)
        rows = sb("rows", [1, N_ROWS, P], F32)
        cols = sb("cols", [P, N_COLS], F32)
        omu = sb("omu", [P, 2], F32)
        bcast = sb("bcast", [P, 3, P], F32)
        ident = sb("ident", [P, P], F32)
        ident_b = sb("ident_b", [P, P], BF16)
        ones_row = sb("ones_row", [1, P], F32)
        ones_b = sb("ones_b", [3, P], BF16)
        bias_row = sb("bias_row", [1, 3, 3 * P], BF16)
        bias_left = sb("bias_left", [1, 2, 3 * P], F32)
        bias_parts = sb("bias_parts", [3, 3 * P], BF16)
        stats = sb("stats", [P, TILES, 6], F32)
        mv = sb("mv", [P, TILES, 2], F32)
        veps = sb("veps", [P, TILES], F32)
        std = sb("std", [P, TILES], F32)
        rstd = sb("rstd", [P, TILES], F32)
        mpart = sb("mpart", [P, ROWS * KC], F32)
        nmax = sb("nmax", [P, ROWS], F32)
        nmax_r = sb("nmax_r", [P, 2, ROWS], F32)
        nmax_p = sb("nmax_p", [P, ROWS, 3], BF16)
        o_tok = sb("o_tok", [P, TPC * HG, VW], F32)
        rden = sb("rden", [P, TPC * HG], F32)

        scratch = [nc.dram_tensor("k_scratch", (3, P, S), BF16, kind="Internal").ap(),
                   nc.dram_tensor("q_scratch", (3, P, S), BF16, kind="Internal").ap()]

        x_loaded = [sem(f"x_loaded_{c}") for c in range(CHUNKS)]
        w_loaded = sem("w_loaded")
        rows_loaded = sem("rows_loaded")
        trig_loaded = [sem(f"trig_loaded_{c}") for c in range(CHUNKS)]
        late_loaded = sem("late_loaded")
        pool_step = sem("pool_step")
        ident_ready = sem("ident_ready")
        zeroed = sem("zeroed")
        v_unit_cleared = sem("v_unit_cleared")
        rows_done = sem("rows_done")
        late_turned = sem("late_turned")
        late_done = sem("late_done")
        vectors_spread = sem("vectors_spread")
        weights_done = sem("weights_done")
        vectors_done = sem("vectors_done")
        dve_step = sem("dve_step")
        var_ready = sem("var_ready")
        std_ready = sem("std_ready")
        xn_ready = sem("xn_ready")
        turned = sem("turned")
        turned_copied = sem("turned_copied")
        proj_ready = sem("proj_ready")
        comb_ready = sem("comb_ready")
        hi_ready = sem("hi_ready")
        resid_ready = sem("resid_ready")
        mid_ready = sem("mid_ready")
        lo_ready = sem("lo_ready")
        v_ready = sem("v_ready")
        v_used = sem("v_used")
        v_biased = sem("v_biased")
        scratch_written = sem("scratch_written")
        stack_loading = sem("stack_loading")
        first_head_loading = sem("first_head_loading")
        stacks_ready = sem("stacks_ready")
        sm_ready = sem("sm_ready")
        sm_free = sem("sm_free")
        ring_ready = sem("ring_ready")
        ring_taken = sem("ring_taken")
        pv_done = sem("pv_done")
        v_unit_ready = sem("v_unit_ready")
        o_copied = sem("o_copied")
        o_turned = sem("o_turned")
        o_taken = sem("o_taken")
        rden_ready = sem("rden_ready")
        o_done = sem("o_done")
        max_step = sem("max_step")
        qkv_ready = sem("qkv_ready")
        qkv_copied = sem("qkv_copied")
        prod_ready = sem("prod_ready")
        pe_summed = sem("pe_summed")
        dve_summed = sem("dve_summed")
        hbias_ready = sem("hbias_ready")
        he_ready = sem("he_ready")
        ctx_ready = sem("ctx_ready")
        xb_ready = sem("xb_ready")
        op_ready = sem("op_ready")
        bias_step = sem("bias_step")
        parts_spread = sem("parts_spread")
        x_new = sem("x_new")
        mixed = sem("mixed")
        wr_mixed = sem("wr_mixed")
        k_ready = sem("k_ready")
        r_ready = sem("r_ready")
        gate_ready = sem("gate_ready")
        relu_ready = sem("relu_ready")
        act_ready = sem("act_ready")
        kv_ready = sem("kv_ready")
        stored = sem("stored")

        MSTEPS = 6

        def turn_bank(c):
            return psum[:, c % 2, :]

        def proj_bank(n):
            return psum[:, 2 + n % 2, :]

        def swap_bank(n):
            return psum[:, 4 + n % 2, :]

        def out_bank(c):
            return psum[:, 6 + c % 2, :]

        def qkv_bank(n):
            return psum[:, n % 2, 0:3 * P]

        def hs_banks(c):
            return psum[:, 2 + 2 * (c % 2):4 + 2 * (c % 2), :].rearrange("p b t -> p (b t)")

        items = []
        for c in range(CHUNKS + 1):
            if c < CHUNKS:
                items += [("qk", TPC * c + i) for i in range(TPC)]
            if c >= 1:
                items += [("pv", TPC * (c - 1) + i) for i in range(TPC)]

        def dve_tiles(kind, c):
            return {"qk": (2, 1, 1, 0), "pv": (1, 1, 1, 1)}[kind][c]

        def summed_by_dve(kind, n):
            return n % TPC >= TPC - dve_tiles(kind, n // TPC)

        def scores_of(n):
            if summed_by_dve("qk", n):
                return hs_raw[:, (n // TPC) % 2, n % TPC - 2, :]
            return hs_banks(n // TPC)[:, (n % TPC) * H * H:(n % TPC + 1) * H * H]

        def sums_before(i, by_dve):
            return sum(summed_by_dve(*it) == by_dve for it in items[:i + 1])

        def item(unit, t, j):
            more = sum((t, j) >= (m, HG - 1) for m in MAX_STEPS) if has_next_unit(unit) else 0
            return unit * ITEMS + (2 + HG * t + j + more)

        def has_next_unit(unit):
            return not (isinstance(unit, int) and unit == UNITS - 1)

        def max_item(unit, half):
            if isinstance(unit, int) and unit == 0:
                return half
            return unit * ITEMS + (2 + HG * MAX_STEPS[half] + HG - 1 + half - ITEMS)

        def slot(unit, t, j):
            return item(0 if has_next_unit(unit) else UNITS - 1, t, j) % SLOTS

        def sm_banks(kc):
            return psum[:, SLOTS + 2 * kc:SLOTS + 2 + 2 * kc, :].rearrange("p b t -> p (b t)")

        acc = psum[:, 7, :]

        def max_rows(bank):
            return psum[MROW:MROW + 3, bank, :].bitcast(BF16)

        def max_slot(unit, half):
            first = isinstance(unit, int) and unit == 0
            return (half if first else item(0, MAX_STEPS[half], HG - 1) - 1) % SLOTS

        def turned_slot(last):
            return ((TOTAL_ITEMS if last else item(0, TURN_STEP, HG - 1)) + 1) % SLOTS

        def k_cols(unit, j, first, n):
            return kst[:, bass.ds(((unit // CHUNKS) % 2) * (HG * S) + (j * S + first), n)]

        def q_cols(unit, j, first, n):
            return qflat[:, bass.ds(((unit // CHUNKS) % 2) * (HG * S) + (unit % CHUNKS) * CHUNK + (j * S + first), n)]

        def max_work(unit, t, has_next, has_second, has_before):
            ahead = STEPS - LEAD
            if t >= ahead:
                return [(unit + 2, t - ahead)] if has_second else []
            if not has_before:
                rest = ROWS - FIRST_LEAD
                return [(unit + 1, FIRST_LEAD + k) for k in range(-(-t * rest // ahead), -(-(t + 1) * rest // ahead))]
            return [(unit + 1, t + LEAD)] if has_next else []

        def attention_units(eng, body):
            body(0, True, True, False)
            with eng.Fori(1, UNITS - 2) as unit:
                body(unit, True, True, True)
            body(UNITS - 2, True, False, True)
            body(UNITS - 1, False, False, True)

        block = ctx.enter_context(nc.Block())

        @block.sync
        def _(sp):
            for c in range(CHUNKS):
                src = x_in[c * CHUNK:(c + 1) * CHUNK, :].rearrange("(n p) d -> p n d", p=P)
                sp.dma_start(x[:, c * TPC:(c + 1) * TPC, :], src).then_inc(x_loaded[c], 16)
            for at, v in ((BQ, bq), (BK, bk), (BV, bv), (BP, bp), (B_OUT, b_out), (MU_R, mu_r), (MU_K, mu_k)):
                sp.dma_start(rows[0:1, at, :], v.rearrange("(a d) -> a d", a=1)).then_inc(rows_loaded, 16)
            for i, w in enumerate((wq, wk, wv)):
                sp.dma_start(wa[:, i, :], w).then_inc(w_loaded, 16)
            for c in range(CHUNKS):
                cs = slice(c * CHUNK, (c + 1) * CHUNK)
                sp.dma_start(cos[:, cs], cos_t[:, cs]).then_inc(trig_loaded[c], 16)
                sp.dma_start(sin[:, cs], sin_t[:, cs]).then_inc(trig_loaded[c], 16)
            sp.dma_start(wa[:, 3, :], wp).then_inc(late_loaded, 16)
            sp.dma_start(rows[0:1, B_QKV:N_ROWS, :].rearrange("p k d -> p (k d)"),
                         b_qkv.rearrange("(a d) -> a d", a=1)).then_inc(late_loaded, 16)
            sp.dma_start(wqkv[:], w_qkv).then_inc(late_loaded, 16)
            sp.dma_start(wout[:], w_out).then_inc(late_loaded, 16)
            for i, w in enumerate((w_r, w_k, w_v)):
                sp.dma_start(wf_in[:, i, :], w).then_inc(late_loaded, 16)

            kdst = kst[:].rearrange("p (a j t) -> p a j t", a=2, j=HG)
            qdst = qst[:].rearrange("p a j c t -> p a j (c t)")

            for n in range(2 * CHUNKS):
                c, kq = n // 2, n % 2
                cs = slice(c * CHUNK, (c + 1) * CHUNK)
                sp.wait_ge(hi_ready, n + 1)
                sp.wait_ge(mid_ready, n + 1)
                sp.dma_start(scratch[kq][0:2, :, cs].rearrange("s p t -> p s t"),
                             parts[kq][:, 0:2, cs]).then_inc(scratch_written, 16)
                sp.wait_ge(lo_ready, n + 1)
                sp.dma_start(scratch[kq][2, :, cs], parts[kq][:, 2, cs]).then_inc(scratch_written, 16)
            sp.wait_ge(scratch_written, 2 * CHUNKS * 2 * 16)
            sp.wait_ge(zeroed, 1)
            loads = 0
            for g in range(GROUPS):
                half = g % 2
                if g == 1:
                    sp.wait_ge(zeroed, 2)
                if g >= 2:
                    sp.wait_ge(ring_taken, SLOTS + item((g - 1) * CHUNKS, 0, 0))
                    sp.dma_start(qst[MROW:MROW + 3, half].rearrange("p j c t -> p (j c t)").bitcast(F32),
                                 zero_rows).then_inc(stack_loading, 16)
                    loads += 1
                for j in range(HG):
                    head = slice((g * HG + j) * HD, (g * HG + j + 1) * HD)
                    signal = first_head_loading if g == 0 and j == 0 else stack_loading
                    for first, n, q_part in RUNS:
                        at = slice(HD * first, HD * (first + n))
                        sp.dma_start(kdst[at, half, j], scratch[0][0:n, head, :]).then_inc(signal, 16)
                        sp.dma_start(qdst[at, half, j], scratch[1][q_part:q_part + 1, head, :].to_broadcast(
                            [n, HD, S])).then_inc(signal, 16)
                        loads += 2 if signal is stack_loading else 0
                sp.wait_ge(stack_loading, 16 * loads)
                sp.sem_inc(stacks_ready, 1)
            for c in range(CHUNKS):
                sp.wait_ge(x_new, 3 * CHUNKS + c + 1)
                dst = out[c * CHUNK:(c + 1) * CHUNK, :].rearrange("(n p) d -> p n d", p=P)
                sp.dma_start(dst, x[:, c * TPC:(c + 1) * TPC, :]).then_inc(stored, 16)
            sp.wait_ge(stored, 16 * CHUNKS)

        @block.gpsimd
        def _(pool):
            pool.memset(ident[:], 0.0).then_inc(pool_step, 1)
            pool.memset(ones_row[:], 1.0).then_inc(pool_step, 1)
            pool.wait_ge(pool_step, 2)
            pool.affine_select(out=ident[:], in_=ident[:], compare_op=ALU.not_equal, fill=1.0, base=0,
                               pattern=[[-1, P]], channel_multiplier=1).then_inc(pool_step, 1)
            pool.wait_ge(pool_step, 3)
            pool.tensor_copy(ident_b[:], ident[:]).then_inc(ident_ready, 1)

            def clear_stacks(half):
                cs = slice(half * HG * S // 2, (half + 1) * HG * S // 2)
                pool.memset(kst[:].bitcast(F32)[:, cs], 0.0).then_inc(pool_step, 1)
                pool.memset(qflat.bitcast(F32)[:, cs], 0.0).then_inc(pool_step, 1)
                pool.wait_ge(pool_step, 3 + 2 * (half + 1))
                pool.memset(kst[MROW:MROW + 3, half * HG * S:(half + 1) * HG * S], 1.0).then_inc(zeroed, 1)
                pool.wait_ge(zeroed, half + 1)

            def residual(n):
                c, kq = n // 2, n % 2
                pool.wait_ge(comb_ready, n + 1)
                pool.wait_ge(hi_ready, n + 1)
                if n >= 2:
                    pool.wait_ge(lo_ready, n - 1)
                    pool.wait_ge(mid_ready, n - 1)
                pool.tensor_tensor(resid[:, n % 2, :], comb[:, n % 2, :],
                                   parts[kq][:, 0, c * CHUNK:(c + 1) * CHUNK], ALU.subtract).then_inc(resid_ready, 1)

            def low(n):
                c, kq = n // 2, n % 2
                pool.wait_ge(mid_ready, n + 1)
                pool.tensor_tensor(parts[kq][:, 2, c * CHUNK:(c + 1) * CHUNK], resid[:, n % 2, :],
                                   parts[kq][:, 1, c * CHUNK:(c + 1) * CHUNK], ALU.subtract).then_inc(lo_ready, 1)

            clear_stacks(0)
            for n in range(2 * CHUNKS + 1):
                if n < 2 * CHUNKS:
                    residual(n)
                if n >= 1:
                    low(n - 1)
            clear_stacks(1)
            pool.wait_ge(vectors_done, 1)
            pool.wait_ge(late_done, 1)
            pool.wait_ge(xn_ready, CHUNKS)
            pool.tensor_tensor(x[:], x[:], bcast[:, 1, :].unsqueeze(1).to_broadcast([P, TILES, P]),
                               ALU.add).then_inc(xb_ready, 1)
            pool.wait_ge(v_used, CHUNKS)
            v_group = v_all[:].rearrange("p (g t j e) -> p g t j e", g=GROUPS, t=TILES, j=HG)
            for g in range(GROUPS):
                bias = bcast[:, 0, g * HG * HD:(g + 1) * HG * HD].rearrange("p (j d) -> p j d", j=HG)
                pool.tensor_tensor(v_group[:, g, :, :, 0:HD], v_group[:, g, :, :, 0:HD],
                                   bias.unsqueeze(1).to_broadcast([P, TILES, HG, HD]), ALU.add).then_inc(v_biased, 1)
            pool.wait_ge(v_biased, GROUPS)
            pool.wait_ge(v_unit_cleared, 1)
            with pool.Fori(0, UNITS) as unit:
                for first, n in ((0, TILES - LAG), (TILES - LAG, LAG)):
                    pool.wait_ge(pv_done, unit * STEPS + (RING + first + n - STEPS))
                    pool.tensor_copy(
                        v_unit[:, first:first + n, :, 0:VW],
                        v_all[:, bass.ds((unit // CHUNKS) * (TILES * HG * VW) + first * HG * VW, n * HG * VW)
                              ].rearrange("p (t j e) -> p t j e", t=n, j=HG)).then_inc(v_unit_ready, 1)
            pool.wait_ge(late_loaded, 7 * 16)
            b_row = rows[0:1, B_QKV:N_ROWS, :].rearrange("p k d -> p (k d)")
            pool.memset(ones_b[:], 1.0).then_inc(bias_step, 1)
            pool.tensor_copy(bias_row[:, 0, :], b_row).then_inc(bias_step, 1)
            pool.wait_ge(bias_step, 2)
            pool.tensor_tensor(bias_left[:, 0, :], b_row, bias_row[:, 0, :], ALU.subtract).then_inc(bias_step, 1)
            pool.wait_ge(bias_step, 3)
            pool.tensor_copy(bias_row[:, 1, :], bias_left[:, 0, :]).then_inc(bias_step, 1)
            pool.wait_ge(bias_step, 4)
            pool.tensor_tensor(bias_left[:, 1, :], bias_left[:, 0, :], bias_row[:, 1, :],
                               ALU.subtract).then_inc(bias_step, 1)
            pool.wait_ge(bias_step, 5)
            pool.tensor_copy(bias_row[:, 2, :], bias_left[:, 1, :]).then_inc(bias_step, 1)
            pool.wait_ge(bias_step, 6)
            pool.dma_start(bias_parts[:], bias_row[:]).then_inc(parts_spread, 16)
            pool.wait_ge(xn_ready, 3 * CHUNKS)
            pool.tensor_tensor(x[:], x[:], bcast[:, 2, :].unsqueeze(1).to_broadcast([P, TILES, P]),
                               ALU.add).then_inc(xb_ready, 1)

        @block.scalar
        def _(act):
            act.sem_inc(ring_taken, SLOTS)

            def weights():
                act.wait_ge(w_loaded, 3 * 16)
                for i in range(2):
                    pair = wa[:, i, :].rearrange("p (n two) -> p n two", two=2)
                    swap = wsw[:, i, :].rearrange("p (n two) -> p n two", two=2)
                    act.copy(swap[:, :, 0], pair[:, :, 1])
                    last = act.copy(swap[:, :, 1], pair[:, :, 0])
                last.then_inc(weights_done, 1)

            def late_weights():
                act.wait_ge(late_turned, 1)
                act.copy(bcast[:, 1:3, :].rearrange("p k n -> p (k n)"), swap_bank(1)[:, 0:2 * P])
                act.copy(wfT[:].rearrange("p k n -> p (k n)"), out_bank(1)[:, 0:3 * P]).then_inc(late_done, 1)
                act.wait_ge(vectors_done, 1)
                act.wait_ge(late_done, 1)
                act.activation(wr_mu[:, 0, :], wfT[:, 0, :], ACT.Copy, scale=cols[:, MU_R:MU_R + 1])
                act.activation(wr_mu[:, 1, :], wfT[:, 0, :], ACT.Copy, scale=omu[:, 0:1]).then_inc(wr_mixed, 1)

            def layer_norm(layer):
                act.wait_ge(var_ready, layer + 1)
                act.activation(std[:], veps[:], ACT.Sqrt).then_inc(std_ready, 1)
                if layer == 0:
                    weights()
                for c in range(CHUNKS if layer == 2 else 2):
                    copy_turned(CHUNKS * (layer + (layer + 1) // 2) + c, c)

            def copy_turned(n, c):
                act.wait_ge(turned, n + 1)
                act.copy(xnT[:, 1 + c * CHUNK:1 + (c + 1) * CHUNK], turn_bank(c)).then_inc(turned_copied, 1)

            def split():
                v_dst = v_all[:].rearrange("p (g t j e) -> p t g j e", g=GROUPS, t=TILES, j=HG)
                for n in range(2 * CHUNKS + 1):
                    if n < 2 * CHUNKS:
                        c, kq = n // 2, n % 2
                        act.wait_ge(comb_ready, n + 1)
                        act.copy(parts[kq][:, 0, c * CHUNK:(c + 1) * CHUNK], comb[:, n % 2, :]).then_inc(hi_ready, 1)
                        if kq == 1 and c + 2 < CHUNKS:
                            copy_turned(c + 2, c + 2)
                    if n >= 1:
                        c, kq = (n - 1) // 2, (n - 1) % 2
                        act.wait_ge(resid_ready, n)
                        act.copy(parts[kq][:, 1, c * CHUNK:(c + 1) * CHUNK],
                                 resid[:, (n - 1) % 2, :]).then_inc(mid_ready, 1)
                        if kq == 1:
                            act.wait_ge(v_ready, c + 1)
                            for i in range(TPC):
                                last = act.copy(
                                    v_dst[:, TPC * c + i, :, :, 0:HD],
                                    out_bank(c)[:, i * P:(i + 1) * P].rearrange("p (g j d) -> p g j d", g=GROUPS, j=HG))
                            last.then_inc(v_used, 1)

            def copy_max(unit, half):
                act.wait_ge(ring_ready, max_item(unit, half) + 1)
                act.copy(qst[MROW:MROW + 3, bass.ds((unit // CHUNKS) % 2, 1), 2 * half:2 * half + 2,
                             bass.ds(unit % CHUNKS, 1), :],
                         max_rows(max_slot(unit, half)).rearrange("p (a j c t) -> p a j c t", a=1, j=2, c=1)
                         ).then_inc(ring_taken, 1)

            def copy_acc(unit):
                act.wait_ge(pv_done, unit * STEPS + (STEPS + RING))
                act.copy(o_unit[:], acc).then_inc(o_copied, 1)

            def copy_turned_output(unit, last):
                act.wait_ge(o_turned, unit + 1)
                act.wait_ge(o_done, unit + 1)
                act.copy(o_tok[:], psum[:, turned_slot(last), :].rearrange(
                    "p (s e) -> p s e", e=STRIP)[:, :, 0:VW]).then_inc(o_taken, 1)

            def unit_body(unit, has_next, has_second, has_before):
                for t in range(STEPS):
                    for j in range(HG):
                        if t == TURN_STEP and j == HG - 1 and has_before:
                            copy_turned_output(unit - 1, False)
                        if has_next and t in MAX_STEPS and j == HG - 1:
                            copy_max(unit + 1, MAX_STEPS.index(t))
                        act.wait_ge(ring_ready, item(unit, t, j) + 1)
                        if j == 0:
                            act.wait_ge(pv_done, unit * STEPS + (t + 1))
                        act.activation(probs[:, t % RING, j * CHUNK:(j + 1) * CHUNK], psum[:, slot(unit, t, j), :],
                                       ACT.Exp, scale=SCALE).then_inc(ring_taken, 1)
                    if t == LAG - 1 and has_before:
                        copy_acc(unit - 1)

            def finish_attention(c0):
                for c in range(CHUNKS):
                    copy_turned(c0 + c, c)

            def ffn(f):
                def gates(c):
                    act.wait_ge(r_ready, CHUNKS * f + c + 1)
                    if c >= 2:
                        act.wait_ge(x_new, CHUNKS * (2 * f + 1) + c - 1)
                    act.activation(gate[:, c % 2, :], proj_bank(c), ACT.Sigmoid).then_inc(gate_ready, 1)

                def keys(c):
                    n = CHUNKS * f + c
                    act.wait_ge(k_ready, n + 1)
                    if c >= 2:
                        act.wait_ge(kv_ready, n - 1)
                    act.activation(relu[:, c % 2, :], swap_bank(c), ACT.Relu).then_inc(relu_ready, 1)
                    act.wait_ge(relu_ready, n + 1)
                    act.activation(act2[:, c % 2, :], relu[:, c % 2, :], ACT.Square).then_inc(act_ready, 1)

                for c in range(CHUNKS):
                    if 1 <= c < CHUNKS - 1:
                        copy_turned(CHUNKS * (3 * f + 2) + c + 1, c + 1)
                    for work in (gates, keys) if c == 0 else (keys, gates):
                        work(c)

            def head_attention():
                def copy_qkv(n):
                    act.wait_ge(qkv_ready, n + 1)
                    act.copy(qkv[:, n, :], qkv_bank(n)).then_inc(qkv_copied, 1)

                def exps(n):
                    c = n // TPC
                    if n % TPC == 0:
                        act.wait_ge(hbias_ready, c + 1)
                    for h in range(H):
                        at = (n % TPC) * H + h
                        last = act.activation(he[:, n, h * H:(h + 1) * H], scores_of(n)[:, h * H:(h + 1) * H], ACT.Exp,
                                              scale=SCALE, bias=hbias[:, c, at:at + 1])
                    last.then_inc(he_ready, 1)

                order = [(copy_qkv, n) for n in range(TPC)]
                for c in range(CHUNKS):
                    ahead = [(copy_qkv, n) for n in range(TPC * (c + 1), min(TPC * (c + 2), TILES))]
                    before = [(exps, n) for n in range(TPC * (c - 1), TPC * c)] if c >= 1 else []
                    order += ahead[:2]
                    for k in range(TPC):
                        order += before[k:k + 1] + ahead[2 + k:3 + k]
                order += [(exps, n) for n in range(TILES - TPC, TILES)]
                for work, n in order:
                    work(n)

            layer_norm(0)
            split()
            late_weights()
            copy_max(0, 0)
            copy_max(0, 1)
            attention_units(act, unit_body)
            copy_acc(UNITS - 1)
            copy_turned_output(UNITS - 1, True)
            finish_attention(CHUNKS)
            layer_norm(1)
            ffn(0)
            layer_norm(2)
            head_attention()
            finish_attention(4 * CHUNKS)
            layer_norm(3)
            ffn(1)

        @block.vector
        def _(dve):
            steps = [0]

            def step(ins):
                steps[0] += 1
                ins.then_inc(dve_step, 1)
                return steps[0]

            dve.sem_inc(sm_free, 2)
            dve.sem_inc(o_done, 1)
            dve.memset(xnT[:, 0:1], 0.0)
            dve.memset(v_all[:].rearrange("p (n e) -> p n e", e=VW)[:, :, HD:VW], 1.0)
            dve.memset(v_unit[:], 0.0).then_inc(v_unit_cleared, 1)

            def swap_rows():
                dve.wait_ge(rows_loaded, 7 * 16)
                pair = rows[0:1, BQ:BK + 1, :].rearrange("p k (n two) -> p k n two", two=2)
                swap = rows[0:1, BQ_SWAP:BK_SWAP + 1, :].rearrange("p k (n two) -> p k n two", two=2)
                dve.tensor_copy(swap[:, :, :, 0], pair[:, :, :, 1])
                dve.tensor_copy(swap[:, :, :, 1], pair[:, :, :, 0]).then_inc(rows_done, 1)

            def vectors():
                dve.wait_ge(vectors_spread, 1)
                dve.tensor_copy(bcast[:, 0, :], swap_bank(1)[:, 0:P])
                done = step(dve.tensor_copy(cols[:], out_bank(0)[:, 0:N_COLS]))
                dve.wait_ge(dve_step, done)
                dve.tensor_scalar(omu[:], cols[:, MU_R:MU_K + 1], -1.0, 1.0, ALU.mult, ALU.add).then_inc(vectors_done, 1)

            def mixes(a, c):
                dve.wait_ge(turned_copied, CHUNKS * (3 * a + 2) + c + 1)
                if c >= 2:
                    dve.wait_ge(k_ready, CHUNKS * a + c - 1)
                cur = xnT[:, 1 + c * CHUNK:1 + (c + 1) * CHUNK]
                prev = xnT[:, c * CHUNK:(c + 1) * CHUNK]
                done = step(dve.tensor_scalar(ffn_k[:, c % 2, :], cur, cols[:, MU_K:MU_K + 1], None, ALU.mult))
                dve.wait_ge(dve_step, done)
                dve.scalar_tensor_tensor(out=ffn_k[:, c % 2, :], in0=prev, scalar=omu[:, 1:2],
                                         in1=ffn_k[:, c % 2, :], op0=ALU.mult, op1=ALU.add).then_inc(mixed, 1)

            stats_step = {}

            def statistics(layer, c):
                if c < CHUNKS:
                    if layer == 0:
                        dve.wait_ge(x_loaded[c], 16)
                    else:
                        dve.wait_ge(x_new, CHUNKS * (layer - 1) + c + 1)
                    for n in range(TPC * c, TPC * (c + 1)):
                        stats_step[layer, c] = step(dve.bn_stats(stats[:, n, :], x[:, n, :]))
                if c >= 1:
                    dve.wait_ge(dve_step, stats_step[layer, c - 1])
                    for n in range(TPC * (c - 1), TPC * c):
                        stats_step[layer] = step(dve.bn_aggr(mv[:, n, :], stats[:, n, :]))

            def layer_norm(layer):
                for c in range(CHUNKS + 1) if layer == 0 else (CHUNKS - 1, CHUNKS):
                    statistics(layer, c)
                dve.wait_ge(dve_step, stats_step[layer])
                dve.tensor_scalar(veps[:], mv[:, :, 1], EPS, None, ALU.add).then_inc(var_ready, 1)
                if layer == 0:
                    swap_rows()
                dve.wait_ge(std_ready, layer + 1)
                done = step(dve.reciprocal(rstd[:], std[:]))
                dve.wait_ge(dve_step, done)
                for n in range(TILES):
                    last = dve.tensor_scalar(xn[:, n, :], x[:, n, :], mv[:, n, 0:1], rstd[:, n:n + 1],
                                             ALU.subtract, ALU.mult)
                    if n % TPC == TPC - 1:
                        last.then_inc(xn_ready, 1)
                    if layer == 0 and n == 2 * TPC - 1:
                        vectors()
                    if layer % 2 == 1 and n == 3 * TPC - 1:
                        mixes(layer // 2, 0)

            def projections():
                col = (BK, BQ)

                def combine(n):
                    c, kq = n // 2, n % 2
                    cs = slice(c * CHUNK, (c + 1) * CHUNK)
                    dve.wait_ge(proj_ready, n + 1)
                    if kq == 0:
                        dve.wait_ge(trig_loaded[c], 32)
                    bias = cols[:, col[kq]:col[kq] + 1]
                    if n >= 1:
                        dve.wait_ge(comb_ready, n)
                    dve.scalar_tensor_tensor(out=rope1, in0=proj_bank(n), scalar=bias, in1=cos[:, cs],
                                             op0=ALU.add, op1=ALU.mult)
                    done = step(dve.scalar_tensor_tensor(
                        out=rope2, in0=swap_bank(n), scalar=cols[:, col[kq] + 2:col[kq] + 3],
                        in1=sin[:, cs], op0=ALU.add, op1=ALU.mult))
                    dve.wait_ge(dve_step, done)
                    if n >= 2:
                        dve.wait_ge(resid_ready, n - 1)
                        dve.wait_ge(hi_ready, n - 1)
                    dve.tensor_tensor(comb[:, n % 2, :], rope1, rope2, ALU.add).then_inc(comb_ready, 1)

                for n in range(2 * CHUNKS):
                    combine(n)

            def take_max(unit, r, kc):
                dve.wait_ge(sm_ready, unit * ROWS * KC + (KC * r + kc + 1))
                if r == 0 and kc == 0 and not (isinstance(unit, int) and unit == 0):
                    dve.wait_ge(max_step, unit * MSTEPS - (MSTEPS - 1))
                dve.tensor_reduce(mpart[:, KC * r + kc:KC * r + kc + 1], sm_banks(kc), AX_X,
                                  ALU.max).then_inc(sm_free, 1)

            def max_parts(unit, i):
                def wait_step(k):
                    dve.wait_ge(max_step, unit * MSTEPS + k)

                if i == 0:
                    dve.wait_ge(sm_free, unit * ROWS * KC + (ROWS * KC + 2))
                    dve.tensor_reduce(nmax[:], mpart[:].rearrange("p (r k) -> p r k", k=KC), AX_X, ALU.max,
                                      negate=True).then_inc(max_step, 1)
                if i == 1:
                    wait_step(1)
                    dve.tensor_copy(nmax_p[:, :, 0], nmax[:]).then_inc(max_step, 1)
                if i == 2:
                    wait_step(2)
                    dve.tensor_tensor(nmax_r[:, 0, :], nmax[:], nmax_p[:, :, 0], ALU.subtract).then_inc(max_step, 1)
                if i == 3:
                    wait_step(3)
                    dve.tensor_copy(nmax_p[:, :, 1], nmax_r[:, 0, :]).then_inc(max_step, 1)
                if i == 4:
                    wait_step(4)
                    dve.tensor_tensor(nmax_r[:, 1, :], nmax_r[:, 0, :], nmax_p[:, :, 1],
                                      ALU.subtract).then_inc(max_step, 1)
                if i == 5:
                    wait_step(5)
                    dve.tensor_copy(nmax_p[:, :, 2], nmax_r[:, 1, :]).then_inc(max_step, 1)

            def norm_recip(unit):
                dve.wait_ge(o_taken, unit + 1)
                dve.reciprocal(rden[:].unsqueeze(2), o_tok[:, :, HD:VW]).then_inc(rden_ready, 1)

            def norm_mul(unit):
                dve.wait_ge(rden_ready, unit + 1)
                dve.tensor_tensor(
                    attn[:, bass.ds((unit % CHUNKS) * TPC, TPC), bass.ds((unit // CHUNKS) * (HG * HD), HG * HD)
                         ].rearrange("p q (j d) -> p q j d", j=HG),
                    o_tok[:, :, 0:HD].rearrange("p (q j) d -> p q j d", q=TPC),
                    rden[:].rearrange("p (q j e) -> p q j e", q=TPC, e=1).to_broadcast([P, TPC, HG, HD]),
                    ALU.mult).then_inc(o_done, 1)

            def unit_body(unit, has_next, has_second, has_before):
                for t in range(STEPS):
                    work = max_work(unit, t, has_next, has_second, has_before)
                    for kc in range(KC):
                        for v, r in work[:1]:
                            take_max(v, r, kc)
                        if has_before and t == TURN_STEP + 1 and kc == 0:
                            norm_recip(unit - 1)
                        if has_before and t == TURN_STEP + 1 and kc == 1:
                            norm_mul(unit - 1)
                        k = (t - (STEPS - LEAD)) * KC + kc + 1
                        if has_next and 0 <= k < MSTEPS // 2:
                            max_parts(unit + 1, 2 * k)
                            max_parts(unit + 1, 2 * k + 1)
                    for v, r in work[1:]:
                        for kc in range(KC):
                            take_max(v, r, kc)

            def attention():
                for r in range(ROWS):
                    for kc in range(KC):
                        take_max(0, r, kc)
                for i in range(MSTEPS):
                    max_parts(0, i)
                for r in range(FIRST_LEAD):
                    for kc in range(KC):
                        take_max(1, r, kc)
                attention_units(dve, unit_body)
                norm_recip(UNITS - 1)
                norm_mul(UNITS - 1)

            def head_attention():
                head = qkv.rearrange("p n (h e) -> p n h e", h=H)
                done = {}

                def wait_summed(i):
                    if summed_by_dve(*items[i]):
                        dve.wait_ge(dve_summed, sums_before(i, True))
                    else:
                        dve.wait_ge(pe_summed, sums_before(i, False))

                def products(i, kind, n):
                    buf = i % RING
                    if i >= RING:
                        wait_summed(i - RING)
                    if kind == "qk":
                        dve.wait_ge(qkv_copied, n + 1)
                        shape = [P, HD, H, H]
                        in0 = head[:, n, :, 0:HD].rearrange("p h d -> p d h").unsqueeze(3).to_broadcast(shape)
                        in1 = head[:, n, :, HD:2 * HD].rearrange("p g d -> p d g").unsqueeze(2).to_broadcast(shape)
                        dst = prod[:, buf, :].rearrange("p (d h g) -> p d h g", h=H, g=H)
                    else:
                        dve.wait_ge(he_ready, n + 1)
                        shape = [P, H, H, HD]
                        in0 = he[:, n, :].rearrange("p (h g) -> p g h", h=H).unsqueeze(3).to_broadcast(shape)
                        in1 = head[:, n, :, 2 * HD:3 * HD].unsqueeze(2).to_broadcast(shape)
                        dst = prod[:, buf, :].rearrange("p (g h d) -> p g h d", g=H, h=H)
                    dve.tensor_tensor(dst, in0, in1, ALU.mult).then_inc(prod_ready, 1)

                def sums(i, kind, n):
                    dve.wait_ge(prod_ready, i + 1)
                    c = n // TPC
                    if kind == "qk":
                        if c >= 2:
                            dve.wait_ge(he_ready, TPC * (c - 1))
                        dve.tensor_reduce(scores_of(n), prod[:, i % RING, :].rearrange("p (d s) -> p s d", d=HD),
                                          AX_X, ALU.add).then_inc(dve_summed, 1)
                        return
                    if c >= 1:
                        dve.wait_ge(ctx_ready, c)
                    dve.tensor_reduce(ctx_raw[:, n % TPC, :], prod[:, i % RING, :].rearrange("p (g s) -> p s g", g=H),
                                      AX_X, ALU.add).then_inc(dve_summed, 1)

                def maxima(i, c):
                    mine = TPC - dve_tiles("qk", c)
                    wait_summed(i - dve_tiles("qk", c))
                    got = step(dve.tensor_reduce(hmax[:, c, 0:mine * H], hs_banks(c)[:, 0:mine * H * H].rearrange(
                        "p (s g) -> p s g", g=H), AX_X, ALU.max, negate=True))
                    if mine < TPC:
                        wait_summed(i)
                        got = step(dve.tensor_reduce(
                            hmax[:, c, mine * H:], hs_raw[:, c % 2, mine - 2:, :].rearrange(
                                "p n (h g) -> p (n h) g", g=H), AX_X, ALU.max, negate=True))
                    dve.wait_ge(dve_step, got)
                    dve.tensor_scalar(hbias[:, c, :], hmax[:, c, :], SCALE, None, ALU.mult).then_inc(hbias_ready, 1)

                def denominators(c):
                    if c >= 1:
                        dve.wait_ge(ctx_ready, c)
                    got = step(dve.tensor_reduce(hden[:, c, :], he[:, c * TPC:(c + 1) * TPC, :].rearrange(
                        "p n (h g) -> p (n h) g", h=H), AX_X, ALU.add))
                    dve.wait_ge(dve_step, got)
                    done[c] = step(dve.reciprocal(hrden[:], hden[:, c, :]))

                def divide(i, c):
                    mine = TPC - dve_tiles("pv", c)
                    dve.wait_ge(dve_step, done[c])
                    for raw, a, b, last in ((out_bank(c), 0, mine, i - dve_tiles("pv", c)),
                                            (ctx_raw.rearrange("p n d -> p (n d)"), mine, TPC, i)):
                        wait_summed(last)
                        div = dve.tensor_tensor(
                            attn[:, c * TPC + a:c * TPC + b, :].rearrange("p n (h d) -> p (n h) d", h=H),
                            raw[:, a * P:b * P].rearrange("p (s d) -> p s d", d=HD),
                            hrden[:, a * H:b * H].unsqueeze(2).to_broadcast([P, (b - a) * H, HD]), ALU.mult)
                    div.then_inc(ctx_ready, 1)

                for i in range(len(items) + 2):
                    if i < len(items):
                        products(i, *items[i])
                        if i >= 1 and summed_by_dve(*items[i - 1]):
                            sums(i - 1, *items[i - 1])
                    if i == len(items):
                        sums(i - 1, *items[i - 1])
                    kind, n = items[i - 2] if i >= 2 else (None, 0)
                    if n % TPC == TPC - 1:
                        if kind == "qk":
                            maxima(i - 2, n // TPC)
                        else:
                            divide(i - 2, n // TPC)
                    if i < len(items) and items[i][0] == "pv" and items[i][1] % TPC == TPC - 1:
                        denominators(items[i][1] // TPC)

            def output_projection(a):
                dve.wait_ge(xb_ready, a + 1)
                for c in range(CHUNKS):
                    dve.wait_ge(op_ready, CHUNKS * a + c + 1)
                    xc = x[:, c * TPC:(c + 1) * TPC, :].rearrange("p n d -> p (n d)")
                    dve.tensor_tensor(xc, out_bank(c), xc, ALU.add).then_inc(x_new, 1)
                    if c >= 1:
                        statistics(2 * a + 1, c - 1)

            def ffn(a):
                def gated(c):
                    dve.wait_ge(kv_ready, CHUNKS * a + c + 1)
                    dve.wait_ge(gate_ready, CHUNKS * a + c + 1)
                    done = step(dve.tensor_tensor(gate[:, c % 2, :], out_bank(c), gate[:, c % 2, :], ALU.mult))
                    dve.wait_ge(dve_step, done)
                    xc = x[:, c * TPC:(c + 1) * TPC, :].rearrange("p n d -> p (n d)")
                    dve.tensor_tensor(xc, gate[:, c % 2, :], xc, ALU.add).then_inc(x_new, 1)

                for c in range(CHUNKS + 1):
                    if 1 <= c < CHUNKS:
                        mixes(a, c)
                    if c >= 1:
                        gated(c - 1)
                    if c >= 2 and a == 0:
                        statistics(2, c - 2)

            layer_norm(0)
            projections()
            attention()
            output_projection(0)
            layer_norm(1)
            ffn(0)
            layer_norm(2)
            head_attention()
            output_projection(1)
            layer_norm(3)
            ffn(1)

        @block.tensor
        def _(pe):
            pe.sem_inc(pv_done, RING)
            pe.wait_ge(ident_ready, 1)

            def vectors():
                pe.wait_ge(rows_done, 1)
                for i in range(N_COLS):
                    pe.transpose(out_bank(0)[:, i:i + 1], rows[0:1, i, :], ident[0:1, 0:1])
                pe.matmul(swap_bank(1)[:, 0:P], ones_row[:], rows[0:1, BV, :], start=True,
                          stop=True).then_inc(vectors_spread, 1)

            def late_weights():
                pe.wait_ge(late_loaded, 7 * 16)
                pe.wait_ge(v_used, CHUNKS)
                pe.wait_ge(comb_ready, 2 * CHUNKS)
                for i in range(3):
                    pe.transpose(out_bank(1)[:, i * P:(i + 1) * P], wf_in[:, i, :], ident[:])
                for i, at in enumerate((BP, B_OUT)):
                    last = pe.matmul(swap_bank(1)[:, i * P:(i + 1) * P], ones_row[:], rows[0:1, at, :],
                                     start=True, stop=True)
                last.then_inc(late_turned, 1)
                pe.wait_ge(late_done, 1)

            def turn(tile_of, n, c):
                if c >= 2:
                    pe.wait_ge(turned_copied, n - 1)
                for i in range(TPC):
                    last = pe.transpose(turn_bank(c)[:, i * P:(i + 1) * P], tile_of(TPC * c + i), ident[:])
                last.then_inc(turned, 1)

            def turn_layer_2():
                for c in range(CHUNKS):
                    pe.wait_ge(xn_ready, CHUNKS * 2 + c + 1)
                    turn(lambda i: xn[:, i, :], CHUNKS * 3 + c, c)

            def projections():
                def turn_chunk(c):
                    pe.wait_ge(xn_ready, c + 1)
                    turn(lambda i: xn[:, i, :], c, c)

                w = (wa[:, 1, :], wa[:, 0, :])
                w_v = wa[:, 2, :]
                turn_chunk(0)
                turn_chunk(1)
                pe.wait_ge(weights_done, 1)
                pe.wait_ge(vectors_done, 1)
                for c in range(CHUNKS):
                    pe.wait_ge(turned_copied, c + 1)
                    xc = xnT[:, 1 + c * CHUNK:1 + (c + 1) * CHUNK]
                    for kq in range(2):
                        n = 2 * c + kq
                        if n >= 2:
                            pe.wait_ge(comb_ready, n - 1)
                        pe.matmul(proj_bank(n), w[kq], xc, start=True, stop=True)
                        pe.matmul(swap_bank(n), wsw[:, 1 - kq, :], xc, start=True,
                                  stop=True).then_inc(proj_ready, 1)
                    if c + 2 < CHUNKS:
                        turn_chunk(c + 2)
                    if c >= 2:
                        pe.wait_ge(v_used, c - 1)
                    for i in range(TPC):
                        last = pe.matmul(out_bank(c)[:, i * P:(i + 1) * P], xc[:, i * P:(i + 1) * P], w_v,
                                         start=True, stop=True)
                    last.then_inc(v_ready, 1)

            def max_scores(unit, r, kc):
                j, qt = r // TPC, r % TPC
                pe.wait_ge(sm_free, unit * ROWS * KC + (KC * r + kc + 1))
                for i in range(KW // CHUNK):
                    last = pe.matmul(sm_banks(kc)[:, i * CHUNK:(i + 1) * CHUNK], q_cols(unit, j, qt * P, P),
                                     k_cols(unit, j, kc * KW + i * CHUNK, CHUNK), start=True, stop=True)
                last.then_inc(sm_ready, 1)

            def scores(unit, t, j):
                pe.wait_ge(ring_taken, item(unit, t, j) + 1)
                pe.matmul(psum[:, slot(unit, t, j), :], k_cols(unit, j, t * P, P), q_cols(unit, j, 0, CHUNK),
                          start=True, stop=True).then_inc(ring_ready, 1)

            def product_v(unit, t):
                if t == 0:
                    pe.wait_ge(v_unit_ready, unit * 2 + 1)
                if t == STEPS - LAG:
                    pe.wait_ge(v_unit_ready, unit * 2 + 2)
                pe.wait_ge(ring_taken, item(unit, t, HG - 1) + (1 + SLOTS))
                for j in range(HG):
                    last = pe.matmul(acc[STRIP * j:STRIP * (j + 1), :], v_unit[:, t, j, :],
                                     probs[:, t % RING, j * CHUNK:(j + 1) * CHUNK],
                                     start=(t == 0), stop=(t == STEPS - 1))
                last.then_inc(pv_done, 1)

            def turn_output(unit, last_unit):
                pe.wait_ge(o_copied, unit + 1)
                pe.wait_ge(ring_taken, TOTAL_ITEMS - 1 + SLOTS if last_unit
                           else item(unit + 1, TURN_STEP, HG - 1) + (SLOTS - 1))
                for q in range(TPC):
                    last = pe.transpose(psum[:, turned_slot(last_unit), q * P:(q + 1) * P],
                                        o_unit[:, q * P:(q + 1) * P], ident[:])
                last.then_inc(o_turned, 1)

            def turn_max(unit, half):
                if half == 0:
                    pe.wait_ge(max_step, unit * MSTEPS + MSTEPS)
                pe.wait_ge(ring_taken, max_item(unit, half) + 1)
                for i in range(ROWS // 2):
                    last = pe.transpose(max_rows(max_slot(unit, half))[:, i * P:(i + 1) * P],
                                        nmax_p[:, half * (ROWS // 2) + i, :], ident_b[:])
                last.then_inc(ring_ready, 1)

            def unit_body(unit, has_next, has_second, has_before):
                for t in range(STEPS):
                    work = max_work(unit, t, has_next, has_second, has_before)
                    if t == STEPS - LEAD and has_second:
                        pe.wait_ge(stacks_ready, (unit + 2) // CHUNKS + 1)
                    for v, r in work[:1]:
                        max_scores(v, r, 0)
                    if t == TURN_STEP + 1 and has_before:
                        pe.wait_ge(o_taken, unit)
                    scores(unit, t, 0)
                    scores(unit, t, 1)
                    scores(unit, t, 2)
                    for v, r in work[:1]:
                        max_scores(v, r, 1)
                    if has_next and t in MAX_STEPS:
                        turn_max(unit + 1, MAX_STEPS.index(t))
                    if t >= LAG:
                        if t == LAG and has_before:
                            pe.wait_ge(o_copied, unit)
                        product_v(unit, t - LAG)
                    elif has_before:
                        product_v(unit - 1, t + (STEPS - LAG))
                    for v, r in work[1:]:
                        max_scores(v, r, 0)
                        max_scores(v, r, 1)
                    if t == TURN_STEP and has_before:
                        turn_output(unit - 1, False)
                    scores(unit, t, 3)

            def attention():
                for r in range(ROWS):
                    if r == 0:
                        pe.wait_ge(zeroed, 1)
                        pe.wait_ge(first_head_loading, 2 * len(RUNS) * 16)
                    if r == TPC:
                        pe.wait_ge(stacks_ready, 1)
                    for kc in range(KC):
                        max_scores(0, r, kc)
                for r in range(FIRST_LEAD):
                    for kc in range(KC):
                        max_scores(1, r, kc)
                turn_max(0, 0)
                turn_max(0, 1)
                pe.wait_ge(ring_taken, SLOTS + 2)
                attention_units(pe, unit_body)
                for t in range(STEPS - LAG, STEPS):
                    product_v(UNITS - 1, t)
                turn_output(UNITS - 1, True)

            def head_qkv(n):
                if n < 2:
                    pe.wait_ge(turned_copied, 4 * CHUNKS)
                else:
                    pe.wait_ge(qkv_copied, n - 1)
                first = 1 + n * P
                pe.matmul(qkv_bank(n), xnT[:, first:first + P], wqkv[:], start=True, stop=False)
                pe.matmul(qkv_bank(n), ones_b[:], bias_parts[:], start=False, stop=True).then_inc(qkv_ready, 1)

            def head_attention():
                for n in range(TPC):
                    head_qkv(n)
                for i, (kind, n) in enumerate(items):
                    if kind == "qk" and n + TPC < TILES:
                        head_qkv(n + TPC)
                    if summed_by_dve(kind, n):
                        continue
                    c = n // TPC
                    if kind == "qk":
                        if n % TPC == 0 and c >= 2:
                            pe.wait_ge(he_ready, TPC * (c - 1))
                        dst, terms = hs_banks(c)[:, (n % TPC) * H * H:(n % TPC + 1) * H * H], HD
                    else:
                        if n % TPC == 0 and c >= 2:
                            pe.wait_ge(ctx_ready, c - 1)
                        dst, terms = out_bank(c)[:, (n % TPC) * P:(n % TPC + 1) * P], H
                    pe.wait_ge(prod_ready, i + 1)
                    w = H * H * HD // terms
                    for k in range(terms):
                        last = pe.matmul(dst, ident[:], prod[:, i % RING, k * w:(k + 1) * w],
                                         start=(k == 0), stop=(k == terms - 1))
                    last.then_inc(pe_summed, 1)

            def output_projection(a):
                if a == 0:
                    pe.wait_ge(o_done, UNITS + 1)
                for c in range(CHUNKS):
                    if a == 1:
                        pe.wait_ge(ctx_ready, c + 1)
                    turn(lambda i: attn[:, i, :], CHUNKS * (3 * a + 1) + c, c)
                for c in range(CHUNKS):
                    pe.wait_ge(turned_copied, CHUNKS * (3 * a + 1) + c + 1)
                    if c >= 2:
                        pe.wait_ge(x_new, CHUNKS * 2 * a + c - 1)
                    for i in range(TPC):
                        first = 1 + (TPC * c + i) * P
                        last = pe.matmul(out_bank(c)[:, i * P:(i + 1) * P], xnT[:, first:first + P],
                                         (wa[:, 3, :], wout[:])[a], start=True, stop=True)
                    last.then_inc(op_ready, 1)

            def ffn(a):
                def turn_chunk(c):
                    layer = 2 * a + 1
                    pe.wait_ge(xn_ready, CHUNKS * layer + c + 1)
                    turn(lambda i: xn[:, i, :], CHUNKS * (3 * a + 2) + c, c)

                def keys(c):
                    pe.wait_ge(mixed, CHUNKS * a + c + 1)
                    if c >= 2:
                        pe.wait_ge(relu_ready, CHUNKS * a + c - 1)
                    pe.matmul(swap_bank(c), wfT[:, 1, :], ffn_k[:, c % 2, :], start=True,
                              stop=True).then_inc(k_ready, 1)

                def gates(c):
                    pe.wait_ge(turned_copied, CHUNKS * (3 * a + 2) + c + 1)
                    if c >= 2:
                        pe.wait_ge(gate_ready, CHUNKS * a + c - 1)
                    for i in range(TPC):
                        for k in range(2):
                            first = (TPC * c + i) * P + 1 - k
                            last = pe.matmul(proj_bank(c)[:, i * P:(i + 1) * P], xnT[:, first:first + P],
                                             wr_mu[:, k, :], start=(k == 0), stop=(k == 1))
                    last.then_inc(r_ready, 1)

                def values(c):
                    pe.wait_ge(act_ready, CHUNKS * a + c + 1)
                    if c >= 2:
                        pe.wait_ge(x_new, CHUNKS * (2 * a + 1) + c - 1)
                    for i in range(TPC):
                        last = pe.matmul(out_bank(c)[:, i * P:(i + 1) * P], act2[:, c % 2, i * P:(i + 1) * P],
                                         wfT[:, 2, :], start=True, stop=True)
                    last.then_inc(kv_ready, 1)

                if a == 0:
                    pe.wait_ge(wr_mixed, 1)
                turn_chunk(0)
                turn_chunk(1)
                for c in range(CHUNKS):
                    if c == 0:
                        gates(c)
                        keys(c)
                    else:
                        keys(c)
                        gates(c)
                    if c + 2 < CHUNKS:
                        turn_chunk(c + 2)
                    values(c)

            vectors()
            projections()
            late_weights()
            attention()
            output_projection(0)
            ffn(0)
            turn_layer_2()
            pe.wait_ge(parts_spread, 16)
            head_attention()
            output_projection(1)
            ffn(1)


def rope_tables():
    inv_freq = (np.float32(1.0) / np.float32(ROPE_BASE) ** (np.arange(0, HD, 2, dtype=np.float32) / np.float32(HD)))
    freqs = np.arange(S, dtype=np.float32)[:, None] * inv_freq.astype(np.float32)
    cos = np.repeat(np.cos(freqs), 2, axis=-1).T
    sin = np.repeat(np.sin(freqs), 2, axis=-1).T
    sign = np.where(np.arange(HD) % 2 == 0, np.float32(-1.0), np.float32(1.0))[:, None]
    return (np.ascontiguousarray(np.tile(cos, (H, 1)).astype(np.float32)),
            np.ascontiguousarray(np.tile(sin * sign, (H, 1)).astype(np.float32)))


COS, SIN = rope_tables()
ZERO_ROWS = np.zeros((3, HG * S // 2), np.float32)

_INS = ['L0_attn_a_x', 'L0_attn_a_Wq', 'L0_attn_a_bq', 'L0_attn_a_Wk', 'L0_attn_a_bk', 'L0_attn_a_Wv',
        'L0_attn_a_bv', 'L0_attn_a_Wp', 'L0_attn_a_bp', 'L0_attn_b_W_qkv', 'L0_attn_b_b_qkv',
        'L0_attn_b_W_out', 'L0_attn_b_b_out', 'L0_ffn_W_r', 'L0_ffn_W_k', 'L0_ffn_W_v', 'L0_ffn_mu_r',
        'L0_ffn_mu_k']


def kernel(**inputs):
    import concourse.bacc as _bacc
    from concourse.bass_utils import run_bass_kernel_spmd as _run

    nc = _bacc.Bacc("TRN2", target_bir_lowering=False, num_devices=1)
    arrays, args = {}, []
    named = {n: np.ascontiguousarray(inputs[n]) for n in _INS}
    named['L0_attn_a_x'] = named['L0_attn_a_x'].reshape(S, P)
    named.update(rope_cos=COS, rope_sin=SIN, zero_rows=ZERO_ROWS)
    for name, a in named.items():
        arrays[f"in_{name}"] = a
        args.append(nc.dram_tensor(f"in_{name}", a.shape, mybir.dt.from_np(a.dtype), kind="ExternalInput").ap())
    args.append(nc.dram_tensor("out_x", (S, P), F32, kind="ExternalOutput").ap())
    build(nc, *args)
    r = _run(nc, [arrays], core_ids=[0])
    return r.results[0]["out_x"].reshape(1, S, P)
```
